# Optimizing a Trainium2 kernel written in Bass

```python
import numpy as np
import jax
import jax.numpy as jnp

def _softmax(x, axis=-1):
    return jax.nn.softmax(x, axis=axis)

def _gelu(x):
    return jax.nn.gelu(x, approximate=True)

def _silu(x):
    return jax.nn.silu(x)

def _sigmoid(x):
    return jax.nn.sigmoid(x)

def _layernorm(x, axis=-1, eps=1e-05):
    m = jnp.mean(x, axis=axis, keepdims=True)
    v = jnp.var(x, axis=axis, keepdims=True)
    return (x - m) / jnp.sqrt(v + eps)

def _scatter_add(tgt, idx, src, axis=0):
    return tgt.at[idx].add(src)

def _segment_sum(src, seg, n):
    return jax.ops.segment_sum(src, seg, n)
kernel_name = 'mk_gps_d1_gnn_r8_5c8d10'

def setup_inputs(seed: int=0):
    np.random.seed(seed)
    _w = jnp.asarray

    def _rec_inputs():
        import jax
        import jax.numpy as jnp
        _gk = jax.random.key(seed)
        x = -6.415e-05 + 1 * jax.random.normal(jax.random.fold_in(_gk, 1), (1250, 512), jnp.float32)
        src = jax.random.randint(jax.random.fold_in(_gk, 2), (40000,), 0, 1250, jnp.int32)
        dst = jax.random.randint(jax.random.fold_in(_gk, 3), (40000,), 0, 1250, jnp.int32)
        _o = jnp.argsort(dst, stable=True)
        src = src[_o]
        dst = dst[_o]
        edge_weight1 = -0.00598325 + 0.997157 * jax.random.normal(jax.random.fold_in(_gk, 12), (40000, 1), jnp.float32)
        return (x, src, dst, edge_weight1)
    x, src, dst, edge_weight1 = _rec_inputs()

    def _L0_gnn_setup():
        import jax, jax.numpy as jnp
        import numpy as np
        N, D, E, L = (2500, 512, 20000, 4)
        BN_EPS = 1e-05

        def _gine_layer(x, src, dst, edge_attr, eps, We, be, W1, b1, gamma, beta, W2, b2):
            e = edge_attr @ We + be
            m = jax.nn.relu(x[src] + e)
            agg = jax.ops.segment_sum(m, dst, num_segments=x.shape[0])
            h = ((1.0 + eps) * x + agg) @ W1 + b1
            mu = jnp.mean(h, axis=0)
            var = jnp.mean(jnp.square(h - mu), axis=0)
            h = (h - mu) * jax.lax.rsqrt(var + BN_EPS) * gamma + beta
            h = jax.nn.relu(h)
            return jax.nn.relu(h @ W2 + b2)
        key = jax.random.key(seed)
        ks = jax.random.split(key, 10)
        x = jax.random.normal(ks[0], (N, D), dtype=jnp.float32)
        edge_index = jax.random.randint(ks[1], (2, E), 0, N, dtype=jnp.int64)
        edge_attr = jax.random.normal(ks[2], (E, 1), dtype=jnp.float32)
        s1 = 1.0 / np.sqrt(D)
        params = {'eps': jnp.zeros((L,), jnp.float32), 'We': jax.random.normal(ks[3], (L, 1, D), jnp.float32) * 1.0, 'be': jnp.zeros((L, D), jnp.float32), 'W1': jax.random.normal(ks[4], (L, D, D), jnp.float32) * s1, 'b1': jnp.zeros((L, D), jnp.float32), 'gamma': jnp.ones((L, D), jnp.float32), 'beta': jnp.zeros((L, D), jnp.float32), 'W2': jax.random.normal(ks[5], (L, D, D), jnp.float32) * s1, 'b2': jnp.zeros((L, D), jnp.float32)}
        return {'x': x, 'edge_index': edge_index, 'edge_attr': edge_attr, **params}
    _L0_gnn_all = _L0_gnn_setup()
    _L0_gnn_in = {k: v for k, v in _L0_gnn_all.items() if k in ('eps', 'We', 'be', 'W1', 'b1', 'gamma', 'beta', 'W2', 'b2')}
    del _L0_gnn_all

    def _L0_mix_setup():
        import jax, jax.numpy as jnp
        import numpy as np
        B, S, DM = (4, 1024, 512)
        H = 8
        D = DM // H

        def _feature_map(t):
            return jax.nn.elu(t) + 1.0
        key = jax.random.key(seed)
        ks = jax.random.split(key, 9)
        s = 1.0 / np.sqrt(DM)
        x = jax.random.normal(ks[0], (B, S, DM), dtype=jnp.float32)
        Wq = jax.random.normal(ks[1], (DM, DM), dtype=jnp.float32) * s
        bq = jnp.zeros((DM,), dtype=jnp.float32)
        Wk = jax.random.normal(ks[2], (DM, DM), dtype=jnp.float32) * s
        bk = jnp.zeros((DM,), dtype=jnp.float32)
        Wv = jax.random.normal(ks[3], (DM, DM), dtype=jnp.float32) * s
        bv = jnp.zeros((DM,), dtype=jnp.float32)
        Wp = jax.random.normal(ks[4], (DM, DM), dtype=jnp.float32) * s
        bp = jnp.zeros((DM,), dtype=jnp.float32)
        return {'x': x, 'Wq': Wq, 'bq': bq, 'Wk': Wk, 'bk': bk, 'Wv': Wv, 'bv': bv, 'Wp': Wp, 'bp': bp}
    _L0_mix_all = _L0_mix_setup()
    _L0_mix_in = {k: v for k, v in _L0_mix_all.items() if k in ('Wq', 'bq', 'Wk', 'bk', 'Wv', 'bv', 'Wp', 'bp')}
    del _L0_mix_all

    def _L0_ffn_setup():
        import jax, jax.numpy as jnp
        import numpy as np
        B, S, D, F, E = (4, 256, 512, 256, 8)
        key = jax.random.key(seed)
        k = jax.random.split(key, 5)
        x = jax.random.normal(k[0], (B, S, D), dtype=jnp.float32)
        Ws = jax.random.normal(k[1], (D, E), dtype=jnp.float32) * 0.02
        bs = jnp.zeros((E,), dtype=jnp.float32)
        W1 = jax.random.normal(k[2], (E, D, F), dtype=jnp.float32) * 0.02
        b1 = jnp.zeros((E, F), dtype=jnp.float32)
        W2 = jax.random.normal(k[3], (E, F, D), dtype=jnp.float32) * 0.02
        b2 = jnp.zeros((E, D), dtype=jnp.float32)
        return {'x': x, 'Ws': Ws, 'bs': bs, 'W1': W1, 'b1': b1, 'W2': W2, 'b2': b2}
    _L0_ffn_all = _L0_ffn_setup()
    _L0_ffn_in = {k: v for k, v in _L0_ffn_all.items() if k in ('Ws', 'bs', 'W1', 'b1', 'W2', 'b2')}
    del _L0_ffn_all
    return {'x': x, 'src': src, 'dst': dst, 'edge_weight1': edge_weight1, 'L0_gnn_eps': _L0_gnn_in['eps'], 'L0_gnn_We': _L0_gnn_in['We'], 'L0_gnn_be': _L0_gnn_in['be'], 'L0_gnn_W1': _L0_gnn_in['W1'], 'L0_gnn_b1': _L0_gnn_in['b1'], 'L0_gnn_gamma': _L0_gnn_in['gamma'], 'L0_gnn_beta': _L0_gnn_in['beta'], 'L0_gnn_W2': _L0_gnn_in['W2'], 'L0_gnn_b2': _L0_gnn_in['b2'], 'L0_mix_Wq': _L0_mix_in['Wq'], 'L0_mix_bq': _L0_mix_in['bq'], 'L0_mix_Wk': _L0_mix_in['Wk'], 'L0_mix_bk': _L0_mix_in['bk'], 'L0_mix_Wv': _L0_mix_in['Wv'], 'L0_mix_bv': _L0_mix_in['bv'], 'L0_mix_Wp': _L0_mix_in['Wp'], 'L0_mix_bp': _L0_mix_in['bp'], 'L0_ffn_Ws': _L0_ffn_in['Ws'], 'L0_ffn_bs': _L0_ffn_in['bs'], 'L0_ffn_W1': _L0_ffn_in['W1'], 'L0_ffn_b1': _L0_ffn_in['b1'], 'L0_ffn_W2': _L0_ffn_in['W2'], 'L0_ffn_b2': _L0_ffn_in['b2']}

def reference(x, src, dst, edge_weight1, L0_gnn_eps, L0_gnn_We, L0_gnn_be, L0_gnn_W1, L0_gnn_b1, L0_gnn_gamma, L0_gnn_beta, L0_gnn_W2, L0_gnn_b2, L0_mix_Wq, L0_mix_bq, L0_mix_Wk, L0_mix_bk, L0_mix_Wv, L0_mix_bv, L0_mix_Wp, L0_mix_bp, L0_ffn_Ws, L0_ffn_bs, L0_ffn_W1, L0_ffn_b1, L0_ffn_W2, L0_ffn_b2):
    import jax
    import jax.numpy as jnp

    def _L0_gnn_ref(x, edge_index, edge_attr, eps, We, be, W1, b1, gamma, beta, W2, b2):
        import jax, jax.numpy as jnp
        import numpy as np
        N, D, E, L = (2500, 512, 20000, 4)
        BN_EPS = 1e-05

        def _gine_layer(x, src, dst, edge_attr, eps, We, be, W1, b1, gamma, beta, W2, b2):
            e = edge_attr @ We + be
            m = jax.nn.relu(x[src] + e)
            agg = jax.ops.segment_sum(m, dst, num_segments=x.shape[0])
            h = ((1.0 + eps) * x + agg) @ W1 + b1
            mu = jnp.mean(h, axis=0)
            var = jnp.mean(jnp.square(h - mu), axis=0)
            h = (h - mu) * jax.lax.rsqrt(var + BN_EPS) * gamma + beta
            h = jax.nn.relu(h)
            return jax.nn.relu(h @ W2 + b2)
        src, dst = (edge_index[0], edge_index[1])
        for l in range(L):
            x = _gine_layer(x, src, dst, edge_attr, eps[l], We[l], be[l], W1[l], b1[l], gamma[l], beta[l], W2[l], b2[l])
        return x

    def _L0_mix_ref(x, Wq, bq, Wk, bk, Wv, bv, Wp, bp):
        import jax, jax.numpy as jnp
        import numpy as np
        B, S, DM = (4, 1024, 512)
        H = 8
        D = DM // H

        def _feature_map(t):
            return jax.nn.elu(t) + 1.0
        b, s, _ = x.shape
        q = _feature_map(x @ Wq + bq).reshape(b, s, H, D)
        k = _feature_map(x @ Wk + bk).reshape(b, s, H, D)
        v = (x @ Wv + bv).reshape(b, s, H, D)
        kv = jnp.einsum('bshd,bshe->bhde', k, v)
        z = 1.0 / jnp.einsum('bshd,bhd->bsh', q, k.sum(axis=1))
        out = jnp.einsum('bshd,bhde,bsh->bshe', q, kv, z)
        out = out.reshape(b, s, H * D)
        return out @ Wp + bp

    def _L0_ffn_ref(x, Ws, bs, W1, b1, W2, b2):
        import jax, jax.numpy as jnp
        import numpy as np
        B, S, D, F, E = (4, 256, 512, 256, 8)
        Bb, Ss, Dd = x.shape
        xt = x.reshape(-1, Dd)
        logits = xt @ Ws + bs
        probs = jax.nn.softmax(logits, axis=-1)
        prob_max = jnp.max(probs, axis=-1)
        routes = jnp.argmax(probs, axis=-1)
        onehot = jax.nn.one_hot(routes, W1.shape[0], dtype=xt.dtype)

        def expert_ffn(w1, bb1, w2, bb2):
            h = jax.nn.gelu(xt @ w1 + bb1, approximate=False)
            return h @ w2 + bb2
        y = jax.vmap(expert_ffn)(W1, b1, W2, b2)
        out = jnp.einsum('te,etd->td', onehot, y)
        out = out * prob_max[:, None]
        return out.reshape(Bb, Ss, Dd)
    edge_index = jnp.stack([src, dst])
    xn = _layernorm(x, axis=-1)
    x = x + _L0_gnn_ref(xn, edge_index, edge_weight1, L0_gnn_eps, L0_gnn_We, L0_gnn_be, L0_gnn_W1, L0_gnn_b1, L0_gnn_gamma, L0_gnn_beta, L0_gnn_W2, L0_gnn_b2) + _L0_mix_ref(xn[None], L0_mix_Wq, L0_mix_bq, L0_mix_Wk, L0_mix_bk, L0_mix_Wv, L0_mix_bv, L0_mix_Wp, L0_mix_bp)[0]
    x = x + _L0_ffn_ref(_layernorm(x, axis=-1)[None], L0_ffn_Ws, L0_ffn_bs, L0_ffn_W1, L0_ffn_b1, L0_ffn_W2, L0_ffn_b2)[0]
    return x

_drawn_inputs = setup_inputs


def setup_inputs(seed=0):
    import zlib

    import numpy as np

    out = dict(_drawn_inputs(seed))
    spreads = {'L0_gnn_eps': (0.0, 0.8),
     'L0_gnn_be': (0.0, 0.1),
     'L0_gnn_b1': (0.0, 2.0),
     'L0_gnn_gamma': (1.0, 0.2),
     'L0_gnn_beta': (0.0, 0.1),
     'L0_gnn_b2': (0.0, 0.1),
     'L0_mix_bq': (0.0, 2.0),
     'L0_mix_bk': (0.0, 2.0),
     'L0_mix_bv': (0.0, 0.1),
     'L0_mix_bp': (0.0, 0.1),
     'L0_ffn_bs': (0.0, 0.648),
     'L0_ffn_b1': (0.0, 0.8),
     'L0_ffn_b2': (0.0, 0.385)}
    factors = {'L0_mix_Wq': 23.155, 'L0_mix_Wk': 8.0, 'L0_ffn_W1': 3.471, 'L0_ffn_W2': 3.241}
    for name, (base, spread) in spreads.items():
        noise = np.random.default_rng([zlib.crc32(name.encode()), seed]).standard_normal(out[name].shape)
        drawn = base * np.exp(spread * noise) if base else spread * noise
        out[name] = jnp.asarray(drawn.astype(out[name].dtype))
    for name, factor in factors.items():
        out[name] = (out[name] * factor).astype(out[name].dtype)
    return out
```

```python
import concourse.bass as bass
from concourse import mybir
from contextlib import ExitStack


def build_gps_block(nc, io, out):
    f32, i32 = mybir.dt.float32, mybir.dt.int32
    ALU, ACT, AX = mybir.AluOpType, mybir.ActivationFunctionType, mybir.AxisListType

    P = 128
    N, D = io["x"].shape
    E = io["src"].shape[0]
    L = io["L0_gnn_W1"].shape[0]
    NE, _, F = io["L0_ffn_W1"].shape
    HD = D // 8
    EPS = 1e-5
    KD = D // P
    KF = F // P
    NT = -(-N // P)
    LAST = N - (NT - 1) * P
    CUT = [(0, 512), (512, 512), (1024, N - 1024)]
    TILES_OF_CUT = [range(0, 4), range(4, 8), range(8, NT)]
    U = 4
    CE = U * P
    NC = -(-E // CE)
    FULL = E // CE
    TAIL = E - FULL * CE
    assert NC == FULL + 1 and 0 < TAIL <= P and FULL % 3 == 0
    ITER = FULL // 3
    WIN = 32
    NW = -(-N // WIN)
    AW = N + WIN + 2
    FAR = 4000.0
    BIG = 8000.0
    SPANS = [(2 * j, 2) for j in range(NT)] + [(2 * NT + j, 1) for j in range(ITER - 2 * NT)]
    PIECES = len(SPANS)
    OUT_TILES = [range(j * NT // (PIECES - NT), (j + 1) * NT // (PIECES - NT)) for j in range(PIECES - NT)]

    def rows(t):
        return LAST if t == NT - 1 else P

    with ExitStack() as ctx:
        def sb(name, shape, dt=f32):
            return ctx.enter_context(nc.sbuf_tensor(name, shape, dt))

        def sem(name):
            return ctx.enter_context(nc.semaphore(name))

        table = nc.dram_tensor("x_table", [N, D], f32).ap()

        ring = sb("ring", [P, 6 * U * D])
        gathered = ring[:, 0:3 * U * D].rearrange("p (k u d) -> p k u d", k=3, u=U)
        message = ring[:, 3 * U * D:].rearrange("p (k u d) -> p k u d", k=3, u=U)
        xrow = ring[:, 0:NT * D].rearrange("p (t d) -> p t d", t=NT)
        xplus = ring[:, NT * D:2 * NT * D].rearrange("p (t d) -> p t d", t=NT)
        ew1 = ring[:, 0:NE * KD * F].rearrange("p (e k f) -> p e k f", e=NE, k=KD)
        onehot = sb("onehot", [P, (FULL * U + 1) * WIN])
        oh = onehot[:, :].rearrange("p (t j) -> p t j", j=WIN)
        ew2 = onehot[:, 0:NE * KF * D].rearrange("p (e k f) -> p e k f", e=NE, k=KF)
        aggT = sb("aggT", [P, KD, AW])
        hT = [aggT[:, 2 * b:2 * b + 2, 0:N] for b in range(2)]
        xT = sb("xT", [P, KD, N])
        zT = sb("zT", [P, KD, N])
        zflat = zT[:, :, :].rearrange("p k n -> p (k n)")
        wq = zflat[:, 0:KD * D].rearrange("p (k n) -> p k n", k=KD)
        wk = zflat[:, KD * D:2 * KD * D].rearrange("p (k n) -> p k n", k=KD)
        wp = wq
        bv_bc = zflat[:, 2 * KD * D:2 * KD * D + D]
        w1 = sb("w1", [P, KD, D])
        mixtmp = w1
        w2 = sb("w2", [P, KD, D])
        wv = w2
        mix = sb("mix", [P, NT, D])
        edge_rows = mix[0:NC, 0:7, :]
        relT = mix[:, 8, 0:NC * U].rearrange("p (c u) -> p c u", u=U)
        we_bc = sb("we_bc", [P, D])
        b2rows = we_bc[0:NE, :]
        be_bc = sb("be_bc", [P, D])
        bp_bc = be_bc
        stage = sb("stage", [P, 2, D])
        kvacc = stage[:, 0, :].rearrange("p (a e) -> p a e", e=P)
        xtile = stage[:, 1, :]
        kvblk = sb("kvblk", [P, D])
        ksblk = sb("ksblk", [P, D])
        qkbias = sb("qkbias", [1, 2 * D])
        idxT = sb("idxT", [P, NC + 2, U], i32)
        wT = sb("wT", [P, NC, U])
        remT = sb("remT", [P, NC, U])
        idx_slot = sb("idx_slot", [P, 3, U], i32)
        base_i = sb("base_i", [1, NC], i32)
        left_f = sb("left_f", [1, NC + 1])
        left_i = sb("left_i", [1, 1], i32)
        ident = sb("ident", [P, P])
        iota_i = sb("iota_i", [P, WIN], i32)
        iota = sb("iota", [P, WIN])
        ones = sb("ones", [P, P])
        pad_i = sb("pad_i", [P, 1], i32)
        params_row = sb("params_row", [4 * L * KD + NE * KF, P])
        params = sb("params", [P, 4 * L * KD + NE * KF])
        par = params[:, 0:4 * L * KD].rearrange("p (a q) -> p a q", a=4)
        cur = sb("cur", [P, 4, KD])
        eps_bc = sb("eps_bc", [P, L])
        eps1 = sb("eps1", [P, L])
        stats = sb("stats", [P, NT, 6])
        mv = sb("mv", [P, NT, 2])
        sc = sb("sc", [P, 8, NT])
        edge_sc = sb("edge_sc", [NC, 4])
        ksum = sb("ksum", [P, KD])
        f_oh = sb("f_oh", [P, U, WIN])
        f_rem = sb("f_rem", [P, U])
        ws = sb("ws", [P, KD, NE])
        bs_bc = sb("bs_bc", [P, NE])
        lg = sb("lg", [P, 4, NT, NE])
        gateT = xT[0:NE, 0, :]

        ps = [ctx.enter_context(nc.psum_tensor(f"ps{i}", [P, 512], f32)) for i in range(8)]

        ident_ready = sem("ident_ready")
        iota_made = sem("iota_made")
        pads_ready = sem("pads_ready")
        x_loaded = sem("x_loaded")
        edges_loaded = sem("edges_loaded")
        small_loaded = sem("small_loaded")
        mixw_loaded = sem("mixw_loaded")
        wp_loaded = sem("wp_loaded")
        xtile_loaded = sem("xtile_loaded")
        we_loaded = sem("we_loaded")
        be_loaded = sem("be_loaded")
        bp_loaded = sem("bp_loaded")
        w1_loaded = sem("w1_loaded")
        w2_loaded = sem("w2_loaded")
        ffn_loaded = sem("ffn_loaded")
        b2_loaded = sem("b2_loaded")
        table_stored = [sem(f"table_stored{b}") for b in range(2)]
        out_stored = sem("out_stored")
        dve = sem("dve_steps")
        act_root = sem("act_root")
        root_in = sem("root_in")
        ln_ready = sem("ln_ready")
        xp_ready = sem("xp_ready")
        prepT = sem("prepT")
        prepT_out = sem("prepT_out")
        xnT_ready = sem("xnT_ready")
        edges_ready = sem("edges_ready")
        edgeT = sem("edgeT")
        edgeT_out = sem("edgeT_out")
        idxT_ready = sem("idxT_ready")
        prep_done = sem("prep_done")
        idx_ready = sem("idx_ready")
        gather_go = sem("gather_go")
        got = [sem(f"got{k}") for k in range(3)]
        summed = sem("summed")
        relu_done = sem("relu_done")
        window_done = sem("window_done")
        flushed = sem("flushed")
        slow_idx = sem("slow_idx")
        slow_got = sem("slow_got")
        slow_sum = sem("slow_sum")
        slow_relu = sem("slow_relu")
        slow_oh = sem("slow_oh")
        slow_win = sem("slow_win")
        slow_add = sem("slow_add")
        slow_go = sem("slow_go")
        stats_ready = sem("stats_ready")
        qkv_done = sem("qkv_done")
        mix_t = sem("mix_t")
        mix_exp = sem("mix_exp")
        mix_kv_in = sem("mix_kv_in")
        kv_done = sem("kv_done")
        kv_taken = sem("kv_taken")
        kvblk_ready = sem("kvblk_ready")
        nd_done = sem("nd_done")
        att_ready = sem("att_ready")
        proj_done = sem("proj_done")
        mix_done = sem("mix_done")
        mm1_done = sem("mm1_done")
        shift_ready = sem("shift_ready")
        z_ready = sem("z_ready")
        mm2_done = sem("mm2_done")
        x_ready = sem("x_ready")
        rowT = sem("rowT")
        staged = sem("staged")
        x2_ready = sem("x2_ready")
        lnT = sem("lnT")
        lnT_out = sem("lnT_out")
        logits_done = sem("logits_done")
        l_exp_in = sem("l_exp_in")
        l_exp = sem("l_exp")
        gate_ready = sem("gate_ready")
        gateT_done = sem("gateT_done")
        gateT_out = sem("gateT_out")
        gb_done = sem("gb_done")
        gb_taken = sem("gb_taken")
        h_done = sem("h_done")
        h_ready = sem("h_ready")
        y_done = sem("y_done")
        y_taken = sem("y_taken")

        block = ctx.enter_context(nc.Block())

        NPAR = L * KD

        @block.sync
        def _(sp):
            sp.wait_ge(pads_ready, 1)
            sp.dma_start(xrow[:, 0:NT - 1, :], io["x"][0:(NT - 1) * P, :].rearrange("(t p) d -> p t d", p=P)).then_inc(x_loaded, 16)
            sp.dma_start(xrow[0:LAST, NT - 1, :], io["x"][(NT - 1) * P:N, :]).then_inc(x_loaded, 16)
            sp.wait_ge(pads_ready, 4)
            for j, name in ((0, "src"), (1, "dst"), (2, "edge_weight1")):
                flat = io[name] if name != "edge_weight1" else io[name].rearrange("e a -> (e a)")
                dst = edge_rows[:, j, :] if name == "edge_weight1" else edge_rows[:, j, :].bitcast(i32)
                sp.dma_start(dst[0:FULL, :], flat[0:FULL * CE].rearrange("(c e) -> c e", e=CE)).then_inc(edges_loaded, 16)
                sp.dma_start(dst[FULL:NC, 0:TAIL], flat[FULL * CE:E].rearrange("(c e) -> c e", c=1)).then_inc(edges_loaded, 16)
            for a, name in enumerate(("b1", "gamma", "beta", "b2")):
                sp.dma_start(params_row[a * NPAR:(a + 1) * NPAR, :],
                             io["L0_gnn_" + name].rearrange("l (c p) -> (l c) p", p=P)).then_inc(small_loaded, 16)
            sp.dma_start(params_row[4 * NPAR:, :], io["L0_ffn_b1"].rearrange("e (c p) -> (e c) p", p=P)).then_inc(small_loaded, 16)
            sp.dma_start(eps_bc[:, :], io["L0_gnn_eps"].rearrange("(a l) -> a l", a=1).to_broadcast([P, L])).then_inc(small_loaded, 16)
            sp.dma_start(be_bc[:, :], io["L0_gnn_be"][0:1, :].to_broadcast([P, D])).then_inc(be_loaded, 16)
            sp.dma_start(we_bc[:, :], io["L0_gnn_We"][0, :, :].to_broadcast([P, D])).then_inc(we_loaded, 16)
            sp.dma_start(wq, io["L0_mix_Wq"].rearrange("(k p) n -> p k n", p=P)).then_inc(mixw_loaded, 16)
            sp.dma_start(wk, io["L0_mix_Wk"].rearrange("(k p) n -> p k n", p=P)).then_inc(mixw_loaded, 16)
            sp.dma_start(wv[:, :, :], io["L0_mix_Wv"].rearrange("(k p) n -> p k n", p=P)).then_inc(mixw_loaded, 16)
            sp.dma_start(qkbias[:, 0:D], io["L0_mix_bq"].rearrange("(a n) -> a n", a=1)).then_inc(mixw_loaded, 16)
            sp.dma_start(qkbias[:, D:], io["L0_mix_bk"].rearrange("(a n) -> a n", a=1)).then_inc(mixw_loaded, 16)
            sp.dma_start(bv_bc, io["L0_mix_bv"].rearrange("(a n) -> a n", a=1).to_broadcast([P, D])).then_inc(mixw_loaded, 16)
            for t in range(NT):
                sp.wait_ge(xp_ready, t + 1)
                sp.dma_start(table[t * P:t * P + rows(t), :], xplus[0:rows(t), t, :]).then_inc(table_stored[t % 2], 16)
            sp.dma_start(bp_bc[:, :], io["L0_mix_bp"].rearrange("(a n) -> a n", a=1).to_broadcast([P, D])).then_inc(bp_loaded, 16)
            sp.wait_ge(qkv_done, 3 * NT)
            sp.dma_start(wp, io["L0_mix_Wp"].rearrange("(k p) n -> p k n", p=P)).then_inc(wp_loaded, 16)
            sp.dma_start(w2[:, :, :], io["L0_gnn_W2"][0].rearrange("(k p) n -> p k n", p=P)).then_inc(w2_loaded, 16)
            for t in range(NT):
                if t == 0:
                    sp.wait_ge(kvblk_ready, 1)
                else:
                    sp.wait_ge(mix_done, t)
                sp.dma_start(xtile[0:rows(t), :], io["x"][t * P:t * P + rows(t), :]).then_inc(xtile_loaded, 16)
            sp.wait_ge(mix_done, NT)
            sp.dma_start(w1[:, :, :], io["L0_gnn_W1"][0].rearrange("(k p) n -> p k n", p=P)).then_inc(w1_loaded, 16)
            with sp.Fori(1, L) as l:
                sp.wait_ge(summed, l * NC)
                sp.dma_start(we_bc[:, :], io["L0_gnn_We"].rearrange("l a d -> (l a) d")[bass.ds(l, 1), :].to_broadcast([P, D])).then_inc(we_loaded, 16)
                sp.dma_start(be_bc[:, :], io["L0_gnn_be"][bass.ds(l, 1), :].to_broadcast([P, D])).then_inc(be_loaded, 16)
                sp.wait_ge(mm1_done, l * 4)
                sp.dma_start(w1[:, :, :], io["L0_gnn_W1"].rearrange("l (k p) n -> p (l k) n", p=P)[:, bass.ds(l * KD, KD), :]).then_inc(w1_loaded, 16)
                sp.wait_ge(mm2_done, l * 12)
                sp.dma_start(w2[:, :, :], io["L0_gnn_W2"].rearrange("l (k p) n -> p (l k) n", p=P)[:, bass.ds(l * KD, KD), :]).then_inc(w2_loaded, 16)
                for t in range(NT):
                    sp.wait_ge(staged, (l - 1) * NT + t + 1)
                    sp.dma_start(table[t * P:t * P + rows(t), :], stage[0:rows(t), t % 2, :]).then_inc(table_stored[t % 2], 16)
            sp.wait_ge(mm1_done, (L - 1) * 4 + 1)
            for e in range(NE):
                sp.dma_start(ew1[:, e, :, :], io["L0_ffn_W1"][e].rearrange("(k p) f -> p k f", p=P)).then_inc(ffn_loaded, 16)
                sp.dma_start(ew2[:, e, :, :], io["L0_ffn_W2"][e].rearrange("(k p) f -> p k f", p=P)).then_inc(ffn_loaded, 16)
            sp.dma_start(b2rows, io["L0_ffn_b2"]).then_inc(b2_loaded, 16)
            sp.dma_start(ws[:, :, :], io["L0_ffn_Ws"].rearrange("(k p) e -> p k e", p=P)).then_inc(b2_loaded, 16)
            sp.dma_start(bs_bc[:, :], io["L0_ffn_bs"].rearrange("(a e) -> a e", a=1).to_broadcast([P, NE])).then_inc(b2_loaded, 16)
            for t in range(NT):
                sp.wait_ge(y_taken, (NE - 1) * NT + t + 1)
                sp.dma_start(out[t * P:t * P + rows(t), :], mix[0:rows(t), t, :]).then_inc(out_stored, 16)
            sp.wait_ge(out_stored, NT * 16)

        @block.gpsimd
        def _(gp):
            gp.memset(xrow[:, NT - 1, :], 0.0).then_inc(pads_ready, 1)
            gp.memset(edge_rows[:, 0, :], 0.0).then_inc(pads_ready, 1)
            gp.memset(edge_rows[:, 1, :].bitcast(i32), int(FAR)).then_inc(pads_ready, 1)
            gp.memset(edge_rows[:, 2, :], 0.0).then_inc(pads_ready, 1)
            gp.memset(ident[:, :], 0.0).then_inc(iota_made, 1)
            gp.memset(ones[:, :], 1.0).then_inc(iota_made, 1)
            gp.iota(iota_i[:, :], [[1, WIN]], base=0, channel_multiplier=0).then_inc(iota_made, 1)
            gp.wait_ge(iota_made, 3)
            gp.affine_select(out=ident[:, :], in_=ident[:, :], compare_op=ALU.not_equal, fill=1.0, base=0,
                             pattern=[[-1, P]], channel_multiplier=1).then_inc(ident_ready, 1)

            def gather(k, u, done):
                gp.indirect_dma_start(out=gathered[:, k, u, :], out_offset=None, in_=table[:, :],
                                      in_offset=bass.IndirectOffsetOnAxis(ap=idx_slot[:, k, u:u + 1], axis=0)
                                      ).then_inc(done, 16)

            def messages(l):
                for b in range(2):
                    gp.wait_ge(table_stored[b], (l + 1) * (NT // 2) * 16)
                gp.wait_ge(idx_ready, l * NC + 3)
                gp.sem_inc(gather_go)
                with gp.Fori(0, ITER) as i:
                    for k in range(3):
                        gp.wait_ge(idx_ready, l * NC + i * 3 + k + 1)
                        gp.sem_inc(gather_go)
                        for u in range(U):
                            gather(k, u, got[k])
                gp.wait_ge(idx_ready, l * NC + FULL + 1)
                gp.sem_inc(gather_go)
                gather(0, 0, got[0])
                left = gp.value_load(left_i[0:1, 0:1], min_val=0, max_val=1)
                with gp.If(left > 0):
                    with gp.Fori(0, NC) as c:
                        gp.wait_ge(slow_idx, l * NC + c + 1)
                        gp.sem_inc(gather_go)
                        for u in range(U):
                            gather(0, u, slow_got)

            gp.wait_ge(prep_done, 1)
            gp.wait_ge(prepT, NT)
            gp.sem_inc(gather_go)
            messages(0)
            with gp.Fori(1, L) as l:
                messages(l)

        @block.vector
        def _(v):
            n = [0]

            def step(ins):
                ins.then_inc(dve, 1)
                n[0] += 1
                v.wait_ge(dve, n[0])

            def root_of_var(mvv, cnt, s):
                step(v.tensor_scalar(sc[:, 0, 0:cnt], mvv, EPS, None, ALU.add))
                v.sem_inc(root_in)
                v.wait_ge(act_root, s)
                step(v.reciprocal(sc[:, 2, 0:cnt], sc[:, 1, 0:cnt]))
                step(v.tensor_tensor(sc[:, 4, 0:cnt], sc[:, 0, 0:cnt], sc[:, 2, 0:cnt], ALU.mult))
                step(v.tensor_tensor(sc[:, 5, 0:cnt], sc[:, 4, 0:cnt], sc[:, 2, 0:cnt], ALU.mult))
                step(v.tensor_scalar(sc[:, 6, 0:cnt], sc[:, 5, 0:cnt], -0.5, 1.5, ALU.mult, ALU.add))
                step(v.tensor_tensor(sc[:, 3, 0:cnt], sc[:, 2, 0:cnt], sc[:, 6, 0:cnt], ALU.mult))

            v.wait_ge(x_loaded, 32)
            for t in range(NT):
                step(v.bn_stats(stats[:, t, :], xrow[:, t, :]))
                step(v.bn_aggr(mv[:, t, :], stats[:, t, :]))
            root_of_var(mv[:, :, 1], NT, 1)
            v.wait_ge(be_loaded, 16)
            for t in range(NT):
                ins = v.tensor_scalar(xrow[:, t, :], xrow[:, t, :], mv[:, t, 0:1], sc[:, 3, t:t + 1], ALU.subtract, ALU.mult)
                ins.then_inc(ln_ready, 1)
                v.wait_ge(ln_ready, t + 1)
                v.tensor_tensor(xplus[:, t, :], xrow[:, t, :], be_bc[:, :], ALU.add).then_inc(xp_ready, 1)

            v.wait_ge(edges_loaded, 96)
            step(v.tensor_copy(edge_rows[:, 3, :], edge_rows[:, 0, :].bitcast(i32)))
            step(v.tensor_copy(edge_rows[:, 4, :], edge_rows[:, 1, :].bitcast(i32)))
            step(v.tensor_reduce(edge_sc[:, 0:1], edge_rows[:, 4, :], AX.X, ALU.min))
            step(v.tensor_scalar(edge_rows[:, 5, :], edge_rows[:, 4, :], edge_sc[:, 0:1], None, ALU.subtract))
            step(v.tensor_scalar(edge_rows[:, 6, :], edge_rows[:, 5, :], float(WIN), BIG, ALU.is_lt, ALU.mult))
            step(v.tensor_tensor(edge_rows[:, 6, :], edge_rows[:, 6, :], edge_rows[:, 4, :], ALU.add))
            step(v.tensor_reduce(edge_sc[:, 1:2], edge_rows[:, 6, :], AX.X, ALU.min))
            v.sem_inc(edges_ready)
            v.wait_ge(iota_made, 3)
            step(v.tensor_copy(iota[:, :], iota_i[:, :]))

            def chunked(m):
                return ps[m][:, 0:U * NC].rearrange("p (u c) -> p c u", u=U)

            v.wait_ge(edgeT, 4)
            step(v.tensor_copy(idxT[:, 0:NC, :], chunked(0)))
            step(v.tensor_copy(idxT[:, NC:NC + 2, :], idxT[:, 1:3, :]))
            v.sem_inc(idxT_ready)
            step(v.tensor_copy(wT[:, :, :], chunked(1)))
            step(v.tensor_copy(relT, chunked(2)))
            step(v.tensor_copy(remT[:, :, :], chunked(3)))
            v.wait_ge(edgeT, 5)
            step(v.tensor_copy(base_i[:, :], ps[4][0:1, 0:NC]))
            step(v.tensor_copy(left_f[:, 0:NC], ps[4][0:1, P:P + NC]))
            step(v.tensor_reduce(left_f[:, NC:NC + 1], left_f[:, 0:NC], AX.X, ALU.min))
            step(v.tensor_scalar(left_i[:, :], left_f[:, NC:NC + 1], FAR, None, ALU.is_lt))
            step(v.tensor_copy(params[:, :], ps[5][:, 0:4 * NPAR + NE * KF]))
            nt1 = FULL * U + 1
            rel = mix[:, 8, 0:nt1].unsqueeze(2).to_broadcast([P, nt1, WIN])
            step(v.tensor_tensor(oh, iota[:, :].unsqueeze(1).to_broadcast([P, nt1, WIN]), rel, ALU.is_equal))
            v.wait_ge(small_loaded, 96)
            step(v.tensor_scalar(eps1[:, :], eps_bc[:, :], 1.0, None, ALU.add))
            step(v.memset(aggT[:, :, N:AW], 0.0))
            v.wait_ge(xnT_ready, NT)
            for k in range(KD):
                step(v.tensor_scalar(aggT[:, k, 0:N], xT[:, k, :], eps1[:, 0:1], None, ALU.mult))
            v.sem_inc(flushed)
            v.sem_inc(flushed)
            v.sem_inc(flushed)
            v.sem_inc(prep_done)
            prep_steps = n[0]

            def add_edges(l, k, c, uses, first, tiles=U):
                v.wait_ge(got[k], uses)
                for u in range(tiles):
                    ins = v.scalar_tensor_tensor(out=gathered[:, k, u, :], in0=we_bc[:, :], scalar=wT[:, bass.ds(c, 1), u:u + 1].rearrange("p a b -> p (a b)"),
                                                 in1=gathered[:, k, u, :], op0=ALU.mult, op1=ALU.add)
                ins.then_inc(summed, 1)

            def flush(l, k, c):
                base = v.value_load(base_i[0:1, bass.ds(c, 1)], min_val=0, max_val=N - 1)
                v.wait_ge(window_done, l * NC + c + 4)
                v.wait_ge(flushed, l * (NC + 1) + 3 + c)
                at = aggT[:, :, bass.ds(base, WIN)]
                v.tensor_tensor(at, ps[k][:, 0:KD * WIN].rearrange("p (a b) -> p a b", a=KD), at, ALU.add).then_inc(flushed, 1)

            GOT0 = ITER * U * 16 + 16
            GOT = ITER * U * 16

            def piece(l, lo, count):
                with v.Fori(lo, lo + count) as i:
                    for k in range(3):
                        c = i * 3 + k
                        add_edges(l, k, c, l * (GOT0 if k == 0 else GOT) + i * (U * 16) + U * 16, 0)
                        flush(l, (k + 1) % 3, c - 2)

            def messages(l, beside):
                v.wait_ge(we_loaded, l * 16 + 16)
                add_edges(l, 0, 0, l * GOT0 + U * 16, 0)
                add_edges(l, 1, 1, l * GOT + U * 16, 0)
                add_edges(l, 2, 2, l * GOT + U * 16, 0)
                flush(l, 0, 0)
                if beside:
                    for j, (lo, count) in enumerate(SPANS):
                        if j >= NT:
                            beside(j)
                        first = 1 if j == 0 else 0
                        piece(l, lo + first, count - first)
                        if j < NT:
                            beside(j)
                else:
                    piece(l, 1, ITER - 1)
                add_edges(l, 0, FULL, (l + 1) * GOT0, 0, tiles=1)
                for c in range(FULL - 2, NC):
                    flush(l, c % 3, c)

            def general(l):
                left = v.value_load(left_i[0:1, 0:1], min_val=0, max_val=1)
                with v.If(left > 0):
                    with v.Fori(0, NC) as c:
                        v.wait_ge(slow_got, (l * NC + c + 1) * U * 16)
                        for u in range(U):
                            ins = v.scalar_tensor_tensor(out=gathered[:, 0, u, :], in0=we_bc[:, :], scalar=wT[:, bass.ds(c, 1), u:u + 1].rearrange("p a b -> p (a b)"),
                                                         in1=gathered[:, 0, u, :], op0=ALU.mult, op1=ALU.add)
                        ins.then_inc(slow_sum, 1)
                        v.tensor_copy(f_rem[:, :], remT[:, bass.ds(c, 1), :].rearrange("p a u -> p (a u)")).then_inc(slow_add, 1)
                        with v.Fori(0, NW) as w:
                            done = (l * NC + c) * (2 * NW + 1) + w * 2
                            v.wait_ge(slow_add, done + 1)
                            v.tensor_tensor(f_oh[:, :, :], iota[:, :].unsqueeze(1).to_broadcast([P, U, WIN]),
                                            f_rem[:, :].unsqueeze(2).to_broadcast([P, U, WIN]), ALU.is_equal).then_inc(slow_oh, 1)
                            v.wait_ge(slow_oh, (l * NC + c) * NW + w + 1)
                            v.tensor_scalar(f_rem[:, :], f_rem[:, :], float(WIN), None, ALU.subtract).then_inc(slow_add, 1)
                            v.wait_ge(slow_win, (l * NC + c) * NW + w + 1)
                            at = aggT[:, :, bass.ds(w * WIN, WIN)]
                            v.tensor_tensor(at, ps[0][:, 0:KD * WIN].rearrange("p (a b) -> p a b", a=KD), at, ALU.add).then_inc(slow_add, 1)

            def batch_norm(l, base):
                n0 = [0]

                def bstep(ins):
                    ins.then_inc(dve, 1)
                    n0[0] += 1
                    v.wait_ge(dve, base + n0[0])
                bstep(v.tensor_copy(cur[:, :, :], par[:, :, bass.ds(l * KD, KD)]))
                for fo in range(KD):
                    v.wait_ge(mm1_done, l * 4 + fo + 1)
                    for s, (a, w) in enumerate(CUT):
                        bstep(v.bn_stats(stats[:, s, :], ps[2 + 3 * (fo % 2) + s][:, 0:w]))
                    v.sem_inc(stats_ready)
                    bstep(v.bn_aggr(mv[:, fo, :], stats[:, 0:3, :]))
                    bstep(v.tensor_scalar(sc[:, 0, 0:1], mv[:, fo, 1:2], EPS, None, ALU.add))
                    v.sem_inc(root_in)
                    bstep(v.tensor_tensor(sc[:, 7, fo:fo + 1], mv[:, fo, 0:1], cur[:, 0, fo:fo + 1], ALU.add))
                    bstep(v.tensor_tensor(sc[:, 7, fo:fo + 1], cur[:, 0, fo:fo + 1], sc[:, 7, fo:fo + 1], ALU.subtract))
                    v.wait_ge(act_root, l * 4 + fo + 2)
                    bstep(v.reciprocal(sc[:, 2, 0:1], sc[:, 1, 0:1]))
                    bstep(v.scalar_tensor_tensor(out=sc[:, 5, 0:1], in0=sc[:, 0, 0:1], scalar=sc[:, 2, 0:1], in1=sc[:, 2, 0:1], op0=ALU.mult, op1=ALU.mult))
                    bstep(v.tensor_scalar(sc[:, 6, 0:1], sc[:, 5, 0:1], -0.5, 1.5, ALU.mult, ALU.add))
                    bstep(v.scalar_tensor_tensor(out=sc[:, 3, fo:fo + 1], in0=sc[:, 2, 0:1], scalar=sc[:, 6, 0:1], in1=cur[:, 1, fo:fo + 1], op0=ALU.mult, op1=ALU.mult))
                    bstep(v.scalar_tensor_tensor(out=sc[:, 4, fo:fo + 1], in0=sc[:, 7, fo:fo + 1], scalar=sc[:, 3, fo:fo + 1], in1=cur[:, 2, fo:fo + 1], op0=ALU.mult, op1=ALU.add))
                    v.sem_inc(shift_ready)
                return n0[0]

            def attention(j):
                if j < NT:
                    r = rows(j)
                    for m, (bank, shape, dst) in enumerate(((3, None, None), (4, None, None))):
                        v.wait_ge(qkv_done, 3 * j + m + 1)
                        pr = P if m == 0 else r
                        src = ps[bank][0:pr, :]
                        if m == 0 and r < P:
                            src = src.rearrange("p (c n) -> p c n", n=P)[:, :, 0:r]
                        tmp = mixtmp[0:pr, 0, :]
                        o = mix[0:pr, j, :] if m == 0 else mixtmp[0:pr, 1, :]
                        if m == 0 and r < P:
                            tmp = tmp.rearrange("p (c n) -> p c n", n=P)[:, :, 0:r]
                            o = o.rearrange("p (c n) -> p c n", n=P)[:, :, 0:r]
                        if m == 1 and j > 0:
                            v.wait_ge(kv_done, j)
                        v.tensor_scalar(tmp, src, 0.0, None, ALU.min).then_inc(mix_t, 1)
                        v.wait_ge(mix_exp, 2 * j + m + 1)
                        step(v.scalar_tensor_tensor(out=o, in0=src, scalar=0.0, in1=tmp, op0=ALU.max, op1=ALU.add))
                    v.wait_ge(qkv_done, 3 * j + 3)
                    step(v.tensor_tensor(mixtmp[0:r, 2, :], ps[5][0:r, :], bv_bc[0:r, :], ALU.add))
                    v.sem_inc(mix_kv_in)
                    v.wait_ge(kv_done, j + 1)
                    kvp = ps[6][:, :].rearrange("p (a e) -> p a e", e=P)
                    if j == 0:
                        step(v.tensor_copy(kvacc, kvp))
                        step(v.tensor_copy(ksum[:, :], ps[7][:, 0:KD]))
                    else:
                        step(v.tensor_tensor(kvacc, kvp, kvacc, ALU.add))
                        step(v.tensor_tensor(ksum[:, :], ps[7][:, 0:KD], ksum[:, :], ALU.add))
                    v.sem_inc(kv_taken)
                    if j == NT - 1:
                        step(v.memset(kvblk[:, :], 0.0))
                        step(v.memset(ksblk[:, :], 0.0))
                        for h in range(2):
                            q = slice(h * HD, (h + 1) * HD)
                            step(v.tensor_copy(kvblk[q, :].rearrange("p (a e) -> p a e", e=P)[:, :, q], kvacc[q, :, q]))
                            for a in range(KD):
                                step(v.tensor_scalar(ksblk[q, a * P + h * HD:a * P + (h + 1) * HD], ones[q, 0:HD], ksum[q, a:a + 1], None, ALU.mult))
                        v.sem_inc(kvblk_ready)
                else:
                    for t in OUT_TILES[j - NT]:
                        r = rows(t)
                        num, den = ps[3], ps[4]
                        cols = lambda ap: ap.rearrange("p (c n) -> p c n", n=P)[:, :, 0:r]
                        v.wait_ge(nd_done, t + 1)
                        step(v.reciprocal(cols(mixtmp[:, 3, :]), cols(den[:, :])))
                        step(v.tensor_tensor(cols(mix[:, t, :]), cols(num[:, :]), cols(mixtmp[:, 3, :]), ALU.mult))
                        v.sem_inc(att_ready)
                        v.wait_ge(proj_done, t + 1)
                        if t == 0:
                            v.wait_ge(bp_loaded, 16)
                        step(v.tensor_tensor(mix[0:r, t, :], ps[5][0:r, :], bp_bc[0:r, :], ALU.add))
                        v.wait_ge(xtile_loaded, 16 * (t + 1))
                        step(v.tensor_tensor(mix[0:r, t, :], mix[0:r, t, :], xtile[0:r, :], ALU.add))
                        v.sem_inc(mix_done)

            def stage_rows(l):
                v.wait_ge(be_loaded, l * 16 + 16)
                for t in range(NT):
                    r = rows(t)
                    v.wait_ge(rowT, (l - 1) * NT + t + 1)
                    v.wait_ge(table_stored[t % 2], (l * (NT // 2) + t // 2) * 16)
                    v.tensor_tensor(stage[0:r, t % 2, :], ps[t % 2][0:r, :], be_bc[0:r, :], ALU.add).then_inc(staged, 1)
                for k in range(KD):
                    ins = v.tensor_scalar(aggT[:, k, 0:N], xT[:, k, :], eps1[:, bass.ds(l, 1)], None, ALU.mult)
                    ins.then_inc(flushed, 1) if k == KD - 1 else None

            messages(0, attention)
            general(0)
            before = n[0]
            per = batch_norm(0, before)
            with v.Fori(1, L) as l:
                stage_rows(l)
                messages(l, None)
                general(l)
                batch_norm(l, before + l * per)
            n[0] = before + L * per

            for t in range(NT):
                r = rows(t)
                v.wait_ge(rowT, (L - 1) * NT + t + 1)
                v.tensor_tensor(mix[0:r, t, :], ps[t % 2][0:r, :], mix[0:r, t, :], ALU.add).then_inc(x2_ready, 1)
                v.wait_ge(x2_ready, t + 1)
                step(v.bn_stats(stats[0:r, t, :], mix[0:r, t, :]))
                step(v.bn_aggr(mv[0:r, t, :], stats[0:r, t, :]))
            root_of_var(mv[:, :, 1], NT, L * 4 + 2)
            for t in range(NT):
                r = rows(t)
                if t >= 2:
                    v.wait_ge(lnT, t - 1)
                v.tensor_scalar(stage[0:r, t % 2, :], mix[0:r, t, :], mv[0:r, t, 0:1], sc[0:r, 3, t:t + 1], ALU.subtract, ALU.mult).then_inc(staged, 1)
            v.wait_ge(b2_loaded, 48)
            v.wait_ge(logits_done, NT)
            lgp = ps[6][:, 0:NT * NE].rearrange("p (t e) -> p t e", e=NE)
            lgt = lambda a: lg[:, a, :, :]
            col = lambda a: sc[:, a, :].unsqueeze(2).to_broadcast([P, NT, NE])
            step(v.tensor_tensor(lg[:, 0, 0:NT - 1, :], lgp[:, 0:NT - 1, :], bs_bc[:, :].unsqueeze(1).to_broadcast([P, NT - 1, NE]), ALU.add))
            step(v.memset(lg[:, 0, NT - 1, :], 0.0))
            step(v.tensor_tensor(lg[0:LAST, 0, NT - 1, :], lgp[0:LAST, NT - 1, :], bs_bc[0:LAST, :], ALU.add))
            step(v.tensor_reduce(sc[:, 0, :], lgt(0), AX.X, ALU.max))
            step(v.tensor_tensor(lgt(0), lgt(0), col(0), ALU.subtract))
            v.sem_inc(l_exp_in)
            v.wait_ge(l_exp, 1)
            step(v.tensor_reduce(sc[:, 1, :], lgt(1), AX.X, ALU.add))
            step(v.reciprocal(sc[:, 2, :], sc[:, 1, :]))
            step(v.tensor_tensor(lgt(1), lgt(1), col(2), ALU.mult))
            step(v.tensor_reduce(sc[:, 3, :], lgt(1), AX.X, ALU.max))
            step(v.tensor_tensor(lgt(2), lgt(1), col(3), ALU.is_equal))
            step(v.tensor_scalar(sc[:, 4, 0:NE], iota[:, 0:NE], -1.0, float(NE), ALU.mult, ALU.add))
            step(v.tensor_tensor(lgt(2), lgt(2), sc[:, 4, 0:NE].unsqueeze(1).to_broadcast([P, NT, NE]), ALU.mult))
            step(v.tensor_reduce(sc[:, 5, :], lgt(2), AX.X, ALU.max))
            step(v.tensor_tensor(lgt(2), lgt(2), col(5), ALU.is_equal))
            step(v.tensor_tensor(lgt(3), lgt(2), col(3), ALU.mult))
            v.sem_inc(gate_ready)
            for t in range(NT):
                r = rows(t)
                v.wait_ge(gateT_done, t + 1)
                v.tensor_copy(gateT[:, t * P:t * P + r], ps[t % 2][0:NE, 0:r]).then_inc(gateT_out, 1)
            for t in range(NT):
                r = rows(t)
                v.wait_ge(gb_done, t + 1)
                v.tensor_tensor(mix[0:r, t, :], ps[t % 2][0:r, :], mix[0:r, t, :], ALU.add).then_inc(gb_taken, 1)
            for e in range(NE):
                for t in range(NT):
                    r = rows(t)
                    v.wait_ge(y_done, e * NT + t + 1)
                    if e == 0:
                        v.wait_ge(gb_taken, t + 1)
                    else:
                        v.wait_ge(y_taken, (e - 1) * NT + t + 1)
                    v.scalar_tensor_tensor(out=mix[0:r, t, :], in0=ps[t % 2][0:r, :], scalar=lg[0:r, 3, t, e:e + 1],
                                           in1=mix[0:r, t, :], op0=ALU.mult, op1=ALU.add).then_inc(y_taken, 1)

        @block.scalar
        def _(a):
            def root(s, src, dst):
                a.wait_ge(root_in, s)
                a.activation(dst, src, ACT.Sqrt).then_inc(act_root, 1)

            root(1, sc[:, 0, :], sc[:, 1, :])
            for t in range(NT):
                r = rows(t)
                a.wait_ge(prepT, t + 1)
                a.activation(xT[:, :, t * P:t * P + r], ps[6 + t % 2][:, :].rearrange("p (c n) -> p c n", n=P)[:, :, 0:r], ACT.Copy).then_inc(xnT_ready, 1)
            a.wait_ge(idxT_ready, 1)
            for k in range(3):
                a.activation(idx_slot[:, k, :], idxT[:, k, :], ACT.Copy).then_inc(idx_ready, 1)

            def relu(l, k, c, tiles=U):
                a.wait_ge(summed, l * NC + c + 1)
                a.wait_ge(window_done, l * NC + c + 1)
                a.activation(message[:, k, 0:tiles, :], gathered[:, k, 0:tiles, :], ACT.Relu).then_inc(relu_done, 1)

            def piece(l, lo, count):
                with a.Fori(lo, lo + count) as i:
                    for k in range(3):
                        relu(l, k, i * 3 + k)
                        a.wait_ge(relu_done, l * NC + i * 3 + k + 1)
                        a.activation(idx_slot[:, k, :], idxT[:, bass.ds(i * 3 + k + 3, 1), :].rearrange("p a u -> p (a u)"), ACT.Copy).then_inc(idx_ready, 1)

            def last_chunk(l):
                relu(l, 0, FULL, tiles=1)
                a.wait_ge(relu_done, l * NC + NC)
                a.activation(idx_slot[:, 0, :], idxT[:, 0, :], ACT.Copy).then_inc(idx_ready, 1)

            def general(l):
                left = a.value_load(left_i[0:1, 0:1], min_val=0, max_val=1)
                with a.If(left > 0):
                    with a.Fori(0, NC) as c:
                        a.wait_ge(idx_ready, l * NC + NC + 3)
                        a.activation(idx_slot[:, 0, :], idxT[:, bass.ds(c, 1), :].rearrange("p a u -> p (a u)"), ACT.Copy).then_inc(slow_idx, 1)
                        a.wait_ge(slow_sum, l * NC + c + 1)
                        a.activation(message[:, 0, :, :], gathered[:, 0, :, :], ACT.Relu).then_inc(slow_relu, 1)
                        a.wait_ge(slow_win, (l * NC + c + 1) * NW)
                    a.activation(idx_slot[:, 0, :], idxT[:, 0, :], ACT.Copy)

            def dense(l):
                for fo in range(KD):
                    root(l * 4 + fo + 2, sc[:, 0, 0:1], sc[:, 1, 0:1])
                    a.wait_ge(shift_ready, l * 4 + fo + 1)
                    for s, (lo, w) in enumerate(CUT):
                        a.activation(zT[:, fo, lo:lo + w], ps[2 + 3 * (fo % 2) + s][:, 0:w], ACT.Relu,
                                     bias=sc[:, 4, fo:fo + 1], scale=sc[:, 3, fo:fo + 1]).then_inc(z_ready, 1)
                for s, (lo, w) in enumerate(CUT):
                    for fo in range(KD):
                        g = s * KD + fo
                        a.wait_ge(mm2_done, l * 12 + g + 1)
                        a.activation(xT[:, fo, lo:lo + w], ps[2 + g % 6][:, 0:w], ACT.Relu, bias=cur[:, 3, fo:fo + 1]).then_inc(x_ready, 1)

            for j, (lo, count) in enumerate(SPANS):
                piece(0, lo, count)
                if j < NT:
                    r = rows(j)
                    for m in range(2):
                        pr = P if m == 0 else r
                        tmp = mixtmp[0:pr, 0, :]
                        if m == 0 and r < P:
                            tmp = tmp.rearrange("p (c n) -> p c n", n=P)[:, :, 0:r]
                        a.wait_ge(mix_t, 2 * j + m + 1)
                        a.activation(tmp, tmp, ACT.Exp).then_inc(mix_exp, 1)
            last_chunk(0)
            general(0)
            dense(0)
            with a.Fori(1, L) as l:
                piece(l, 0, ITER)
                last_chunk(l)
                general(l)
                dense(l)

            root(L * 4 + 2, sc[:, 0, :], sc[:, 1, :])
            for t in range(NT):
                r = rows(t)
                a.wait_ge(lnT, t + 1)
                a.activation(zT[:, :, t * P:t * P + r], ps[2 + t % 2][:, :].rearrange("p (c n) -> p c n", n=P)[:, :, 0:r], ACT.Copy).then_inc(lnT_out, 1)
            a.wait_ge(l_exp_in, 1)
            a.activation(lg[:, 1, :, :], lg[:, 0, :, :], ACT.Exp).then_inc(l_exp, 1)
            for e in range(NE):
                if e >= 2:
                    a.wait_ge(y_done, (e - 1) * NT)
                for f in range(KF):
                    for s, (lo, w) in enumerate(CUT):
                        a.wait_ge(h_done, e * 6 + f * 3 + s + 1)
                        a.activation(hT[e % 2][:, f, lo:lo + w], ps[2 + f * 3 + s][:, 0:w], ACT.Gelu,
                                     bias=params[:, 4 * NPAR + e * KF + f:4 * NPAR + e * KF + f + 1]).then_inc(h_ready, 1)

        @block.tensor
        def _(pe):
            def mm(o, lhsT, rhs, start, stop):
                return nc.tensor.matmul(o, lhsT, rhs, start=start, stop=stop)

            for _ in range(3):
                pe.sem_inc(window_done)
            pe.wait_ge(ident_ready, 1)
            for t in range(NT):
                r = rows(t)
                pe.wait_ge(ln_ready, t + 1)
                if t >= 2:
                    pe.wait_ge(xnT_ready, t - 1)
                for c in range(KD):
                    ins = pe.transpose(ps[6 + t % 2][:, c * P:c * P + r], xrow[0:r, t, c * P:(c + 1) * P], ident[0:r, 0:r])
                ins.then_inc(prepT, 1)
            pe.wait_ge(edges_ready, 1)
            for m, row in enumerate((3, 2, 5, 6)):
                for u in range(U):
                    ins = pe.transpose(ps[m][:, u * NC:(u + 1) * NC], edge_rows[:, row, u * P:(u + 1) * P], ident[0:NC, 0:NC])
                ins.then_inc(edgeT, 1)
            pe.transpose(ps[4][0:1, 0:NC], edge_sc[:, 0:1], ident[0:NC, 0:NC])
            pe.transpose(ps[4][0:1, P:P + NC], edge_sc[:, 1:2], ident[0:NC, 0:NC])
            pe.wait_ge(small_loaded, 96)
            npar = 4 * NPAR + NE * KF
            pe.transpose(ps[5][:, 0:npar], params_row[:, :], ident[0:npar, 0:npar]).then_inc(edgeT, 1)
            pe.wait_ge(prep_done, 1)

            def windows(l, k, c, tiles=U):
                pe.wait_ge(relu_done, l * NC + c + 1)
                pe.wait_ge(flushed, l * (NC + 1) + c + 1)
                for q in range(KD):
                    for u in range(tiles):
                        ins = mm(ps[k][:, q * WIN:(q + 1) * WIN], message[:, k, u, q * P:(q + 1) * P],
                                 oh[:, bass.ds(c * U + u, 1), :].rearrange("p a j -> p (a j)"), u == 0, u == tiles - 1)
                ins.then_inc(window_done, 1)

            def piece(l, lo, count):
                with pe.Fori(lo, lo + count) as i:
                    for k in range(3):
                        windows(l, k, i * 3 + k)

            def general(l):
                left = pe.value_load(left_i[0:1, 0:1], min_val=0, max_val=1)
                with pe.If(left > 0):
                    with pe.Fori(0, NC) as c:
                        pe.wait_ge(slow_relu, l * NC + c + 1)
                        pe.sem_inc(slow_go)
                        with pe.Fori(0, NW) as w:
                            pe.wait_ge(slow_oh, (l * NC + c) * NW + w + 1)
                            for q in range(KD):
                                for u in range(U):
                                    ins = mm(ps[0][:, q * WIN:(q + 1) * WIN], message[:, 0, u, q * P:(q + 1) * P], f_oh[:, u, :], u == 0, u == U - 1)
                            ins.then_inc(slow_win, 1)
                    pe.wait_ge(slow_add, (l + 1) * NC * (2 * NW + 1))

            def attention(j):
                if j < NT:
                    r = rows(j)
                    cols = slice(j * P, j * P + r)
                    if j == 0:
                        pe.wait_ge(mixw_loaded, 96)
                    if j > 0:
                        pe.wait_ge(mix_kv_in, j)
                    for c in range(KD):
                        for k in range(KD):
                            mm(ps[3][:, c * P:c * P + r], wq[:, k, c * P:(c + 1) * P], xT[:, k, cols], k == 0, False)
                        ins = mm(ps[3][:, c * P:c * P + r], qkbias[:, c * P:(c + 1) * P], ones[0:1, 0:r], False, True)
                    ins.then_inc(qkv_done, 1)
                    for k in range(KD):
                        mm(ps[4][0:r, :], xT[:, k, cols], wk[:, k, :], k == 0, False)
                    mm(ps[4][0:r, :], ones[0:1, 0:r], qkbias[:, D:], False, True).then_inc(qkv_done, 1)
                    for k in range(KD):
                        ins = mm(ps[5][0:r, :], xT[:, k, cols], wv[:, k, :], k == 0, k == KD - 1)
                    ins.then_inc(qkv_done, 1)
                else:
                    if j == NT:
                        pe.wait_ge(kvblk_ready, 1)
                        pe.wait_ge(wp_loaded, 16)
                    for t in OUT_TILES[j - NT]:
                        r = rows(t)
                        if t > 0:
                            pe.wait_ge(mix_done, t)
                        for bank, blk in ((3, kvblk), (4, ksblk)):
                            for c in range(KD):
                                ins = mm(ps[bank][:, c * P:c * P + r], blk[:, c * P:(c + 1) * P], mix[:, t, c * P:c * P + r], True, True)
                        ins.then_inc(nd_done, 1)
                        pe.wait_ge(att_ready, t + 1)
                        for k in range(KD):
                            ins = mm(ps[5][0:r, :], mix[:, t, k * P:k * P + r], wp[:, k, :], k == 0, k == KD - 1)
                        ins.then_inc(proj_done, 1)

            def key_value(j):
                r = rows(j)
                pe.wait_ge(mix_kv_in, j + 1)
                if j > 0:
                    pe.wait_ge(kv_taken, j)
                for c in range(KD):
                    mm(ps[6][:, c * P:(c + 1) * P], mixtmp[0:r, 1, c * P:(c + 1) * P], mixtmp[0:r, 2, c * P:(c + 1) * P], True, True)
                    ins = mm(ps[7][:, c:c + 1], mixtmp[0:r, 1, c * P:(c + 1) * P], ones[0:r, 0:1], True, True)
                ins.then_inc(kv_done, 1)

            def dense(l):
                pe.wait_ge(flushed, (l + 1) * (NC + 1) + 2)
                pe.wait_ge(w1_loaded, l * 16 + 16)
                for fo in range(KD):
                    if fo >= 2:
                        pe.wait_ge(z_ready, l * 12 + 3 * (fo - 1))
                    for k in range(KD):
                        for s, (lo, w) in enumerate(CUT):
                            ins = mm(ps[2 + 3 * (fo % 2) + s][:, 0:w], w1[:, k, fo * P:(fo + 1) * P], aggT[:, k, lo:lo + w], k == 0, k == KD - 1)
                    ins.then_inc(mm1_done, 1)
                pe.wait_ge(z_ready, (l + 1) * 12)
                pe.wait_ge(w2_loaded, l * 16 + 16)
                for s, (lo, w) in enumerate(CUT):
                    for fo in range(KD):
                        g = s * KD + fo
                        if g >= 6:
                            pe.wait_ge(x_ready, l * 12 + g - 5)
                        for k in range(KD):
                            ins = mm(ps[2 + g % 6][:, 0:w], w2[:, k, fo * P:(fo + 1) * P], zT[:, k, lo:lo + w], k == 0, k == KD - 1)
                        ins.then_inc(mm2_done, 1)
                    if s > 0:
                        rows_of(l, s - 1)
                rows_of(l, len(CUT) - 1)

            def rows_of(l, s):
                pe.wait_ge(x_ready, l * 12 + (s + 1) * KD)
                for t in TILES_OF_CUT[s]:
                    r = rows(t)
                    if t >= 2:
                        free_rows(l, t)
                    for c in range(KD):
                        ins = pe.transpose(ps[t % 2][0:r, c * P:(c + 1) * P], xT[:, c, t * P:t * P + r], ident[:, :])
                    ins.then_inc(rowT, 1)

            def free_rows(l, t):
                if last[0]:
                    pe.wait_ge(x2_ready, t - 1)
                else:
                    pe.wait_ge(staged, l * NT + t - 1)

            last = [False]
            for j, (lo, count) in enumerate(SPANS):
                attention(j)
                piece(0, lo, count)
                if j < NT:
                    key_value(j)
            windows(0, 0, FULL, tiles=1)
            general(0)
            dense(0)
            with pe.Fori(1, L - 1) as l:
                piece(l, 0, ITER)
                windows(l, 0, FULL, tiles=1)
                general(l)
                dense(l)
            last[0] = True
            piece(L - 1, 0, ITER)
            windows(L - 1, 0, FULL, tiles=1)
            general(L - 1)
            dense(L - 1)

            pe.wait_ge(b2_loaded, 48)
            for t in range(NT):
                r = rows(t)
                pe.wait_ge(staged, (L - 1) * NT + t + 1)
                if t >= 2:
                    pe.wait_ge(lnT_out, t - 1)
                for c in range(KD):
                    ins = pe.transpose(ps[2 + t % 2][:, c * P:c * P + r], stage[0:r, t % 2, c * P:(c + 1) * P], ident[0:r, 0:r])
                ins.then_inc(lnT, 1)
            for t in range(NT):
                r = rows(t)
                pe.wait_ge(lnT_out, t + 1)
                for k in range(KD):
                    ins = mm(ps[6][0:r, t * NE:(t + 1) * NE], zT[:, k, t * P:t * P + r], ws[:, k, :], k == 0, k == KD - 1)
                ins.then_inc(logits_done, 1)

            def hidden(e):
                for f in range(KF):
                    for s, (lo, w) in enumerate(CUT):
                        if e > 0:
                            pe.wait_ge(h_ready, (e - 1) * 6 + f * 3 + s + 1)
                    for k in range(KD):
                        for s, (lo, w) in enumerate(CUT):
                            ins = mm(ps[2 + f * 3 + s][:, 0:w], ew1[:, e, k, f * P:(f + 1) * P], zT[:, k, lo:lo + w], k == 0, k == KD - 1)
                            if k == KD - 1:
                                ins.then_inc(h_done, 1)

            pe.wait_ge(ffn_loaded, 2 * NE * 16)
            pe.wait_ge(l_exp_in, 1)
            hidden(0)
            pe.wait_ge(gate_ready, 1)
            for t in range(NT):
                r = rows(t)
                if t >= 2:
                    pe.wait_ge(gateT_out, t - 1)
                pe.transpose(ps[t % 2][0:NE, 0:r], lg[0:r, 3, t, :], ident[0:r, 0:r]).then_inc(gateT_done, 1)
            for t in range(NT):
                r = rows(t)
                if t == 0:
                    pe.wait_ge(gateT_out, NT)
                if t >= 2:
                    pe.wait_ge(gb_taken, t - 1)
                mm(ps[t % 2][0:r, :], gateT[:, t * P:t * P + r], b2rows, True, True).then_inc(gb_done, 1)
            for e in range(NE):
                if e + 1 < NE:
                    hidden(e + 1)
                pe.wait_ge(h_ready, (e + 1) * 6)
                for t in range(NT):
                    r = rows(t)
                    if e == 0 and t < 2:
                        pe.wait_ge(gb_taken, NT)
                    else:
                        pe.wait_ge(y_taken, e * NT + t - 1)
                    for f in range(KF):
                        ins = mm(ps[t % 2][0:r, :], hT[e % 2][:, f, t * P:t * P + r], ew2[:, e, f, :], f == 0, f == KF - 1)
                    ins.then_inc(y_done, 1)


def kernel(**inputs):
    import numpy as _np
    import concourse.bacc as _bacc
    from concourse import mybir as _mybir
    from concourse.bass_utils import run_bass_kernel_spmd as _run

    nc = _bacc.Bacc("TRN2", target_bir_lowering=False, num_devices=1)
    arrays, io = {}, {}
    for name in inputs:
        a = _np.ascontiguousarray(inputs[name])
        arrays[f"in_{name}"] = a
        io[name] = nc.dram_tensor(f"in_{name}", a.shape, _mybir.dt.from_np(a.dtype), kind="ExternalInput").ap()
    shape = inputs["x"].shape
    out = nc.dram_tensor("out_0", shape, _mybir.dt.float32, kind="ExternalOutput").ap()
    build_gps_block(nc, io, out)
    r = _run(nc, [arrays], core_ids=[0])
    return r.results[0]["out_0"]
```

```python
import concourse.bass as bass
from concourse import mybir
from contextlib import ExitStack


def build_gps_block(nc, io, out):
    f32, i32 = mybir.dt.float32, mybir.dt.int32
    ALU, ACT, AX = mybir.AluOpType, mybir.ActivationFunctionType, mybir.AxisListType

    P = 128
    N, D = io["x"].shape
    E = io["src"].shape[0]
    L = io["L0_gnn_W1"].shape[0]
    NE, _, F = io["L0_ffn_W1"].shape
    HD = D // 8
    EPS = 1e-5
    KD = D // P
    KF = F // P
    NT = -(-N // P)
    LAST = N - (NT - 1) * P
    CUT = [(0, 512), (512, 512), (1024, N - 1024)]
    TILES_OF_CUT = [range(0, 4), range(4, 8), range(8, NT)]
    U = 4
    CE = U * P
    NC = -(-E // CE)
    FULL = E // CE
    TAIL = E - FULL * CE
    STEP = 6
    assert NC == FULL + 1 and 0 < TAIL <= P and FULL % STEP == 0
    ITER = FULL // STEP
    WIN = 32
    NW = -(-N // WIN)
    AW = N + WIN + 2
    FAR = 4000.0
    BIG = 8000.0
    OUT_TILES = [range(j * NT // (ITER - NT), (j + 1) * NT // (ITER - NT)) for j in range(ITER - NT)]

    def rows(t):
        return LAST if t == NT - 1 else P

    with ExitStack() as ctx:
        def sb(name, shape, dt=f32):
            return ctx.enter_context(nc.sbuf_tensor(name, shape, dt))

        def sem(name):
            return ctx.enter_context(nc.semaphore(name))

        table = nc.dram_tensor("x_table", [N, D], f32).ap()

        ring = sb("ring", [P, 6 * U * D])
        gathered = ring[:, 0:3 * U * D].rearrange("p (k u d) -> p k u d", k=3, u=U)
        message = ring[:, 3 * U * D:].rearrange("p (k u d) -> p k u d", k=3, u=U)
        xrow = ring[:, 0:NT * D].rearrange("p (t d) -> p t d", t=NT)
        xplus = ring[:, NT * D:2 * NT * D].rearrange("p (t d) -> p t d", t=NT)
        ew1 = ring[:, 0:NE * KD * F].rearrange("p (e k f) -> p e k f", e=NE, k=KD)
        ew2 = sb("ew2", [P, NE, KF, D])
        onehot = sb("onehot", [P, 3, U, WIN])
        aggT = sb("aggT", [P, KD, AW])
        hT = [aggT[:, 2 * b:2 * b + 2, 0:N] for b in range(2)]
        xT = sb("xT", [P, KD, N])
        zT = sb("zT", [P, KD, N])
        zflat = zT[:, :, :].rearrange("p k n -> p (k n)")
        wq = zflat[:, 0:KD * D].rearrange("p (k n) -> p k n", k=KD)
        wk = zflat[:, KD * D:2 * KD * D].rearrange("p (k n) -> p k n", k=KD)
        wp = wq
        bv_bc = zflat[:, 2 * KD * D:2 * KD * D + D]
        w1 = sb("w1", [P, KD, D])
        mixtmp = w1
        w2 = sb("w2", [P, KD, D])
        wv = w2
        mix = sb("mix", [P, NT, D])
        edge_rows = mix[0:NC, 0:7, :]
        we_bc = sb("we_bc", [P, D])
        b2rows = we_bc[0:NE, :]
        be_bc = sb("be_bc", [P, D])
        bp_bc = be_bc
        stage = sb("stage", [P, 2, D])
        kvacc = stage[:, 0, :].rearrange("p (a e) -> p a e", e=P)
        xtile = stage[:, 1, :]
        kvblk = sb("kvblk", [P, D])
        ksblk = sb("ksblk", [P, D])
        q_bias = kvblk[0:1, :]
        k_bias = ksblk[0:1, :]
        parts = sb("parts", [P, 2, D])
        fold = sb("fold", [P, WIN])
        idxT = sb("idxT", [P, NC + 2, U], i32)
        wT = sb("wT", [P, NC, U])
        remT = sb("remT", [P, NC, U])
        relT = sb("relT", [P, NC, U])
        idx_slot = sb("idx_slot", [P, 3, U], i32)
        base_i = sb("base_i", [1, NC], i32)
        left_f = sb("left_f", [1, NC + 1])
        left_i = sb("left_i", [1, 1], i32)
        ident = sb("ident", [P, P])
        iota_i = sb("iota_i", [P, WIN], i32)
        iota = sb("iota", [P, WIN])
        ones = sb("ones", [P, P])
        pad_i = sb("pad_i", [P, 1], i32)
        params_row = sb("params_row", [4 * L * KD + NE * KF, P])
        params = sb("params", [P, 4 * L * KD + NE * KF])
        par = params[:, 0:4 * L * KD].rearrange("p (a q) -> p a q", a=4)
        cur = sb("cur", [P, 4, KD])
        eps_bc = sb("eps_bc", [P, L])
        eps1 = sb("eps1", [P, L])
        stats = sb("stats", [P, NT, 6])
        mv = sb("mv", [P, NT, 2])
        sc = sb("sc", [P, 8, NT])
        edge_sc = sb("edge_sc", [NC, 4])
        ksum = sb("ksum", [P, KD])
        f_oh = sb("f_oh", [P, U, WIN])
        f_rem = sb("f_rem", [P, U])
        ws = sb("ws", [P, KD, NE])
        bs_bc = sb("bs_bc", [P, NE])
        lg = sb("lg", [P, 4, NT, NE])
        gateT = xT[0:NE, 0, :]

        ps = [ctx.enter_context(nc.psum_tensor(f"ps{i}", [P, 512], f32)) for i in range(8)]

        ident_ready = sem("ident_ready")
        iota_made = sem("iota_made")
        pads_ready = sem("pads_ready")
        x_loaded = sem("x_loaded")
        edges_loaded = sem("edges_loaded")
        small_loaded = sem("small_loaded")
        mixw_loaded = sem("mixw_loaded")
        wp_loaded = sem("wp_loaded")
        xtile_loaded = sem("xtile_loaded")
        we_loaded = sem("we_loaded")
        be_loaded = sem("be_loaded")
        bp_loaded = sem("bp_loaded")
        w1_loaded = sem("w1_loaded")
        w2_loaded = sem("w2_loaded")
        ffn_loaded = sem("ffn_loaded")
        b2_loaded = sem("b2_loaded")
        table_stored = [sem(f"table_stored{b}") for b in range(2)]
        out_stored = sem("out_stored")
        dve = sem("dve_steps")
        act_root = sem("act_root")
        root_in = sem("root_in")
        ln_ready = sem("ln_ready")
        xp_ready = sem("xp_ready")
        prepT = sem("prepT")
        prepT_out = sem("prepT_out")
        xnT_ready = sem("xnT_ready")
        edges_ready = sem("edges_ready")
        edgeT = sem("edgeT")
        edgeT_out = sem("edgeT_out")
        idxT_ready = sem("idxT_ready")
        prep_done = sem("prep_done")
        idx_ready = sem("idx_ready")
        gather_go = sem("gather_go")
        got = [sem(f"got{k}") for k in range(3)]
        summed = sem("summed")
        relu_done = sem("relu_done")
        parts_done = sem("parts_done")
        parts_out = sem("parts_out")
        window_done = sem("window_done")
        flushed = sem("flushed")
        slow_idx = sem("slow_idx")
        slow_got = sem("slow_got")
        slow_sum = sem("slow_sum")
        slow_relu = sem("slow_relu")
        slow_oh = sem("slow_oh")
        slow_win = sem("slow_win")
        slow_add = sem("slow_add")
        slow_go = sem("slow_go")
        stats_ready = sem("stats_ready")
        qkv_done = sem("qkv_done")
        mix_t = sem("mix_t")
        mix_exp = sem("mix_exp")
        mix_kv_in = sem("mix_kv_in")
        kv_done = sem("kv_done")
        kv_taken = sem("kv_taken")
        kvblk_ready = sem("kvblk_ready")
        nd_done = sem("nd_done")
        att_ready = sem("att_ready")
        proj_done = sem("proj_done")
        mix_done = sem("mix_done")
        mm1_done = sem("mm1_done")
        shift_ready = sem("shift_ready")
        z_ready = sem("z_ready")
        mm2_done = sem("mm2_done")
        x_ready = sem("x_ready")
        rowT = sem("rowT")
        staged = sem("staged")
        x2_ready = sem("x2_ready")
        lnT = sem("lnT")
        lnT_out = sem("lnT_out")
        logits_done = sem("logits_done")
        l_exp_in = sem("l_exp_in")
        l_exp = sem("l_exp")
        gate_ready = sem("gate_ready")
        gateT_done = sem("gateT_done")
        gateT_out = sem("gateT_out")
        gb_done = sem("gb_done")
        gb_taken = sem("gb_taken")
        h_done = sem("h_done")
        h_ready = sem("h_ready")
        y_done = sem("y_done")
        y_taken = sem("y_taken")

        block = ctx.enter_context(nc.Block())

        NPAR = L * KD

        @block.sync
        def _(sp):
            sp.wait_ge(pads_ready, 1)
            sp.dma_start(xrow[:, 0:NT - 1, :], io["x"][0:(NT - 1) * P, :].rearrange("(t p) d -> p t d", p=P)).then_inc(x_loaded, 16)
            sp.dma_start(xrow[0:LAST, NT - 1, :], io["x"][(NT - 1) * P:N, :]).then_inc(x_loaded, 16)
            sp.wait_ge(pads_ready, 4)
            for j, name in ((0, "src"), (1, "dst"), (2, "edge_weight1")):
                flat = io[name] if name != "edge_weight1" else io[name].rearrange("e a -> (e a)")
                dst = edge_rows[:, j, :] if name == "edge_weight1" else edge_rows[:, j, :].bitcast(i32)
                sp.dma_start(dst[0:FULL, :], flat[0:FULL * CE].rearrange("(c e) -> c e", e=CE)).then_inc(edges_loaded, 16)
                sp.dma_start(dst[FULL:NC, 0:TAIL], flat[FULL * CE:E].rearrange("(c e) -> c e", c=1)).then_inc(edges_loaded, 16)
            for a, name in enumerate(("b1", "gamma", "beta", "b2")):
                sp.dma_start(params_row[a * NPAR:(a + 1) * NPAR, :],
                             io["L0_gnn_" + name].rearrange("l (c p) -> (l c) p", p=P)).then_inc(small_loaded, 16)
            sp.dma_start(params_row[4 * NPAR:, :], io["L0_ffn_b1"].rearrange("e (c p) -> (e c) p", p=P)).then_inc(small_loaded, 16)
            sp.dma_start(eps_bc[:, :], io["L0_gnn_eps"].rearrange("(a l) -> a l", a=1).to_broadcast([P, L])).then_inc(small_loaded, 16)
            sp.dma_start(be_bc[:, :], io["L0_gnn_be"][0:1, :].to_broadcast([P, D])).then_inc(be_loaded, 16)
            sp.dma_start(we_bc[:, :], io["L0_gnn_We"][0, :, :].to_broadcast([P, D])).then_inc(we_loaded, 16)
            sp.dma_start(wq, io["L0_mix_Wq"].rearrange("(k p) n -> p k n", p=P)).then_inc(mixw_loaded, 16)
            sp.dma_start(wk, io["L0_mix_Wk"].rearrange("(k p) n -> p k n", p=P)).then_inc(mixw_loaded, 16)
            sp.dma_start(wv[:, :, :], io["L0_mix_Wv"].rearrange("(k p) n -> p k n", p=P)).then_inc(mixw_loaded, 16)
            sp.dma_start(q_bias, io["L0_mix_bq"].rearrange("(a n) -> a n", a=1)).then_inc(mixw_loaded, 16)
            sp.dma_start(k_bias, io["L0_mix_bk"].rearrange("(a n) -> a n", a=1)).then_inc(mixw_loaded, 16)
            sp.dma_start(bv_bc, io["L0_mix_bv"].rearrange("(a n) -> a n", a=1).to_broadcast([P, D])).then_inc(mixw_loaded, 16)
            for t in range(NT):
                sp.wait_ge(xp_ready, t + 1)
                sp.dma_start(table[t * P:t * P + rows(t), :], xplus[0:rows(t), t, :]).then_inc(table_stored[t % 2], 16)
            sp.dma_start(bp_bc[:, :], io["L0_mix_bp"].rearrange("(a n) -> a n", a=1).to_broadcast([P, D])).then_inc(bp_loaded, 16)
            sp.wait_ge(qkv_done, 3 * NT)
            sp.dma_start(wp, io["L0_mix_Wp"].rearrange("(k p) n -> p k n", p=P)).then_inc(wp_loaded, 16)
            sp.dma_start(w2[:, :, :], io["L0_gnn_W2"][0].rearrange("(k p) n -> p k n", p=P)).then_inc(w2_loaded, 16)
            for t in range(NT):
                if t == 0:
                    sp.wait_ge(kvblk_ready, 1)
                else:
                    sp.wait_ge(mix_done, t)
                sp.dma_start(xtile[0:rows(t), :], io["x"][t * P:t * P + rows(t), :]).then_inc(xtile_loaded, 16)
            sp.wait_ge(mix_done, NT)
            sp.dma_start(w1[:, :, :], io["L0_gnn_W1"][0].rearrange("(k p) n -> p k n", p=P)).then_inc(w1_loaded, 16)
            with sp.Fori(1, L) as l:
                sp.wait_ge(mm1_done, l * KD)
                sp.dma_start(we_bc[:, :], io["L0_gnn_We"].rearrange("l a d -> (l a) d")[bass.ds(l, 1), :].to_broadcast([P, D])).then_inc(we_loaded, 16)
                sp.dma_start(be_bc[:, :], io["L0_gnn_be"][bass.ds(l, 1), :].to_broadcast([P, D])).then_inc(be_loaded, 16)
                sp.dma_start(w1[:, :, :], io["L0_gnn_W1"].rearrange("l (k p) n -> p (l k) n", p=P)[:, bass.ds(l * KD, KD), :]).then_inc(w1_loaded, 16)
                sp.wait_ge(mm2_done, l * 12)
                sp.dma_start(w2[:, :, :], io["L0_gnn_W2"].rearrange("l (k p) n -> p (l k) n", p=P)[:, bass.ds(l * KD, KD), :]).then_inc(w2_loaded, 16)
                for t in range(NT):
                    sp.wait_ge(staged, (l - 1) * NT + t + 1)
                    sp.dma_start(table[t * P:t * P + rows(t), :], stage[0:rows(t), t % 2, :]).then_inc(table_stored[t % 2], 16)
            sp.wait_ge(mm1_done, (L - 1) * 4 + 1)
            for e in range(NE):
                sp.dma_start(ew1[:, e, :, :], io["L0_ffn_W1"][e].rearrange("(k p) f -> p k f", p=P)).then_inc(ffn_loaded, 16)
                sp.dma_start(ew2[:, e, :, :], io["L0_ffn_W2"][e].rearrange("(k p) f -> p k f", p=P)).then_inc(ffn_loaded, 16)
            sp.dma_start(b2rows, io["L0_ffn_b2"]).then_inc(b2_loaded, 16)
            sp.dma_start(ws[:, :, :], io["L0_ffn_Ws"].rearrange("(k p) e -> p k e", p=P)).then_inc(b2_loaded, 16)
            sp.dma_start(bs_bc[:, :], io["L0_ffn_bs"].rearrange("(a e) -> a e", a=1).to_broadcast([P, NE])).then_inc(b2_loaded, 16)
            for t in range(NT):
                sp.wait_ge(y_taken, (NE - 1) * NT + t + 1)
                sp.dma_start(out[t * P:t * P + rows(t), :], mix[0:rows(t), t, :]).then_inc(out_stored, 16)
            sp.wait_ge(out_stored, NT * 16)

        @block.gpsimd
        def _(gp):
            gp.memset(xrow[:, NT - 1, :], 0.0).then_inc(pads_ready, 1)
            gp.memset(edge_rows[:, 0, :], 0.0).then_inc(pads_ready, 1)
            gp.memset(edge_rows[:, 1, :].bitcast(i32), int(FAR)).then_inc(pads_ready, 1)
            gp.memset(edge_rows[:, 2, :], 0.0).then_inc(pads_ready, 1)
            gp.memset(ident[:, :], 0.0).then_inc(iota_made, 1)
            gp.memset(ones[:, :], 1.0).then_inc(iota_made, 1)
            gp.iota(iota_i[:, :], [[1, WIN]], base=0, channel_multiplier=0).then_inc(iota_made, 1)
            gp.wait_ge(iota_made, 3)
            gp.memset(fold[:, :], 0.0).then_inc(iota_made, 1)
            for g in range(U):
                gp.wait_ge(iota_made, 4 + g)
                gp.affine_select(out=fold[:, :], in_=fold[:, :], compare_op=ALU.not_equal, fill=1.0, base=-WIN * g,
                                 pattern=[[-1, WIN]], channel_multiplier=1).then_inc(iota_made, 1)
            gp.affine_select(out=ident[:, :], in_=ident[:, :], compare_op=ALU.not_equal, fill=1.0, base=0,
                             pattern=[[-1, P]], channel_multiplier=1).then_inc(ident_ready, 1)

            def gather(k, u, done):
                gp.indirect_dma_start(out=gathered[:, k, u, :], out_offset=None, in_=table[:, :],
                                      in_offset=bass.IndirectOffsetOnAxis(ap=idx_slot[:, k, u:u + 1], axis=0)
                                      ).then_inc(done, 16)

            def messages(l):
                for b in range(2):
                    gp.wait_ge(table_stored[b], (l + 1) * (NT // 2) * 16)
                gp.wait_ge(idx_ready, l * NC + 3)
                gp.sem_inc(gather_go)
                with gp.Fori(0, ITER) as i:
                    for kk in range(STEP):
                        gp.wait_ge(idx_ready, l * NC + i * STEP + kk + 1)
                        gp.sem_inc(gather_go)
                        for u in range(U):
                            gather(kk % 3, u, got[kk % 3])
                gp.wait_ge(idx_ready, l * NC + FULL + 1)
                gp.sem_inc(gather_go)
                gather(0, 0, got[0])
                left = gp.value_load(left_i[0:1, 0:1], min_val=0, max_val=1)
                with gp.If(left > 0):
                    with gp.Fori(0, NC) as c:
                        gp.wait_ge(slow_idx, l * NC + c + 1)
                        gp.sem_inc(gather_go)
                        for u in range(U):
                            gather(0, u, slow_got)

            gp.wait_ge(prep_done, 1)
            gp.wait_ge(prepT, NT)
            gp.sem_inc(gather_go)
            messages(0)
            with gp.Fori(1, L) as l:
                messages(l)

        @block.vector
        def _(v):
            n = [0]

            def step(ins):
                ins.then_inc(dve, 1)
                n[0] += 1
                v.wait_ge(dve, n[0])

            def root_of_var(mvv, cnt, s):
                step(v.tensor_scalar(sc[:, 0, 0:cnt], mvv, EPS, None, ALU.add))
                v.sem_inc(root_in)
                v.wait_ge(act_root, s)
                step(v.reciprocal(sc[:, 2, 0:cnt], sc[:, 1, 0:cnt]))
                step(v.tensor_tensor(sc[:, 4, 0:cnt], sc[:, 0, 0:cnt], sc[:, 2, 0:cnt], ALU.mult))
                step(v.tensor_tensor(sc[:, 5, 0:cnt], sc[:, 4, 0:cnt], sc[:, 2, 0:cnt], ALU.mult))
                step(v.tensor_scalar(sc[:, 6, 0:cnt], sc[:, 5, 0:cnt], -0.5, 1.5, ALU.mult, ALU.add))
                step(v.tensor_tensor(sc[:, 3, 0:cnt], sc[:, 2, 0:cnt], sc[:, 6, 0:cnt], ALU.mult))

            v.wait_ge(x_loaded, 32)
            for t in range(NT):
                step(v.bn_stats(stats[:, t, :], xrow[:, t, :]))
                step(v.bn_aggr(mv[:, t, :], stats[:, t, :]))
            root_of_var(mv[:, :, 1], NT, 1)
            v.wait_ge(be_loaded, 16)
            for t in range(NT):
                ins = v.tensor_scalar(xrow[:, t, :], xrow[:, t, :], mv[:, t, 0:1], sc[:, 3, t:t + 1], ALU.subtract, ALU.mult)
                ins.then_inc(ln_ready, 1)
                v.wait_ge(ln_ready, t + 1)
                v.tensor_tensor(xplus[:, t, :], xrow[:, t, :], be_bc[:, :], ALU.add).then_inc(xp_ready, 1)

            v.wait_ge(edges_loaded, 96)
            step(v.tensor_copy(edge_rows[:, 3, :], edge_rows[:, 0, :].bitcast(i32)))
            step(v.tensor_copy(edge_rows[:, 4, :], edge_rows[:, 1, :].bitcast(i32)))
            step(v.tensor_reduce(edge_sc[:, 0:1], edge_rows[:, 4, :], AX.X, ALU.min))
            step(v.tensor_scalar(edge_rows[:, 5, :], edge_rows[:, 4, :], edge_sc[:, 0:1], None, ALU.subtract))
            step(v.tensor_scalar(edge_rows[:, 6, :], edge_rows[:, 5, :], float(WIN), BIG, ALU.is_lt, ALU.mult))
            step(v.tensor_tensor(edge_rows[:, 6, :], edge_rows[:, 6, :], edge_rows[:, 4, :], ALU.add))
            step(v.tensor_reduce(edge_sc[:, 1:2], edge_rows[:, 6, :], AX.X, ALU.min))
            v.sem_inc(edges_ready)
            v.wait_ge(iota_made, 3)
            step(v.tensor_copy(iota[:, :], iota_i[:, :]))

            def chunked(m):
                return ps[m][:, 0:U * NC].rearrange("p (u c) -> p c u", u=U)

            v.wait_ge(edgeT, 4)
            step(v.tensor_copy(idxT[:, 0:NC, :], chunked(0)))
            step(v.tensor_copy(idxT[:, NC:NC + 2, :], idxT[:, 1:3, :]))
            v.sem_inc(idxT_ready)
            step(v.tensor_copy(wT[:, :, :], chunked(1)))
            step(v.tensor_copy(relT[:, :, :], chunked(2)))
            step(v.tensor_copy(remT[:, :, :], chunked(3)))
            v.wait_ge(edgeT, 5)
            step(v.tensor_copy(base_i[:, :], ps[4][0:1, 0:NC]))
            step(v.tensor_copy(left_f[:, 0:NC], ps[4][0:1, P:P + NC]))
            step(v.tensor_reduce(left_f[:, NC:NC + 1], left_f[:, 0:NC], AX.X, ALU.min))
            step(v.tensor_scalar(left_i[:, :], left_f[:, NC:NC + 1], FAR, None, ALU.is_lt))
            step(v.tensor_copy(params[:, :], ps[5][:, 0:4 * NPAR + NE * KF]))
            v.wait_ge(small_loaded, 96)
            step(v.tensor_scalar(eps1[:, :], eps_bc[:, :], 1.0, None, ALU.add))
            step(v.memset(aggT[:, :, N:AW], 0.0))
            v.wait_ge(xnT_ready, NT)
            for k in range(KD):
                step(v.tensor_scalar(aggT[:, k, 0:N], xT[:, k, :], eps1[:, 0:1], None, ALU.mult))
            v.sem_inc(flushed)
            v.sem_inc(flushed)
            v.sem_inc(flushed)
            v.sem_inc(slow_add)
            v.sem_inc(prep_done)
            prep_steps = n[0]

            def add_edges(l, k, c, uses, tiles=U):
                v.wait_ge(parts_done, l * NC + c + 1)
                v.tensor_tensor(onehot[:, k, :, :], iota[:, :].unsqueeze(1).to_broadcast([P, U, WIN]),
                                relT[:, bass.ds(c, 1), :].rearrange("p a u -> p (a u)").unsqueeze(2).to_broadcast([P, U, WIN]), ALU.is_equal)
                v.wait_ge(got[k], uses)
                for u in range(tiles):
                    ins = v.scalar_tensor_tensor(out=gathered[:, k, u, :], in0=we_bc[:, :], scalar=wT[:, bass.ds(c, 1), u:u + 1].rearrange("p a b -> p (a b)"),
                                                 in1=gathered[:, k, u, :], op0=ALU.mult, op1=ALU.add)
                ins.then_inc(summed, 1)

            def flush(l, c):
                base = v.value_load(base_i[0:1, bass.ds(c, 1)], min_val=0, max_val=N - 1)
                v.wait_ge(window_done, l * NC + c + 3)
                v.wait_ge(flushed, l * (NC + 1) + 3 + c)
                at = aggT[:, :, bass.ds(base, WIN)]
                v.tensor_tensor(at, ps[2][:, 0:P].rearrange("p (a b) -> p a b", a=KD), at, ALU.add).then_inc(flushed, 1)

            GOT = FULL // 3 * U * 16
            GOT0 = GOT + 16

            def message_step(l, i, first=False):
                for kk in range(STEP):
                    k = kk % 3
                    add_edges(l, k, i * STEP + kk, l * (GOT0 if k == 0 else GOT) + (i * (STEP // 3) + kk // 3 + 1) * (U * 16))
                    if not (first and kk < 2):
                        flush(l, i * STEP + kk - 2)

            def messages(l, beside):
                v.wait_ge(we_loaded, l * 16 + 16)
                if beside:
                    for i in range(ITER):
                        if i >= NT:
                            beside(i)
                        message_step(l, i, first=i == 0)
                        if i < NT:
                            beside(i)
                else:
                    message_step(l, 0, first=True)
                    with v.Fori(1, ITER) as i:
                        message_step(l, i)
                add_edges(l, 0, FULL, (l + 1) * GOT0, tiles=1)
                for c in range(FULL - 2, NC):
                    flush(l, c)

            def general(l):
                left = v.value_load(left_i[0:1, 0:1], min_val=0, max_val=1)
                with v.If(left > 0):
                    with v.Fori(0, NC) as c:
                        v.wait_ge(slow_got, (l * NC + c + 1) * U * 16)
                        for u in range(U):
                            ins = v.scalar_tensor_tensor(out=gathered[:, 0, u, :], in0=we_bc[:, :], scalar=wT[:, bass.ds(c, 1), u:u + 1].rearrange("p a b -> p (a b)"),
                                                         in1=gathered[:, 0, u, :], op0=ALU.mult, op1=ALU.add)
                        ins.then_inc(slow_sum, 1)
                        v.wait_ge(slow_add, (l * NC + c) * (2 * NW + 1) + 1)
                        v.tensor_copy(f_rem[:, :], remT[:, bass.ds(c, 1), :].rearrange("p a u -> p (a u)")).then_inc(slow_add, 1)
                        with v.Fori(0, NW) as w:
                            done = (l * NC + c) * (2 * NW + 1) + w * 2
                            v.wait_ge(slow_add, done + 2)
                            v.tensor_tensor(f_oh[:, :, :], iota[:, :].unsqueeze(1).to_broadcast([P, U, WIN]),
                                            f_rem[:, :].unsqueeze(2).to_broadcast([P, U, WIN]), ALU.is_equal).then_inc(slow_oh, 1)
                            v.wait_ge(slow_oh, (l * NC + c) * NW + w + 1)
                            v.tensor_scalar(f_rem[:, :], f_rem[:, :], float(WIN), None, ALU.subtract).then_inc(slow_add, 1)
                            v.wait_ge(slow_win, (l * NC + c) * NW + w + 1)
                            at = aggT[:, :, bass.ds(w * WIN, WIN)]
                            v.tensor_tensor(at, ps[0][:, 0:KD * WIN].rearrange("p (a b) -> p a b", a=KD), at, ALU.add).then_inc(slow_add, 1)

            def batch_norm(l, base):
                n0 = [0]

                def bstep(ins):
                    ins.then_inc(dve, 1)
                    n0[0] += 1
                    v.wait_ge(dve, base + n0[0])
                bstep(v.tensor_copy(cur[:, :, :], par[:, :, bass.ds(l * KD, KD)]))
                for fo in range(KD):
                    v.wait_ge(mm1_done, l * 4 + fo + 1)
                    for s, (a, w) in enumerate(CUT):
                        bstep(v.bn_stats(stats[:, s, :], ps[2 + 3 * (fo % 2) + s][:, 0:w]))
                    v.sem_inc(stats_ready)
                    bstep(v.bn_aggr(mv[:, fo, :], stats[:, 0:3, :]))
                    bstep(v.tensor_scalar(sc[:, 0, 0:1], mv[:, fo, 1:2], EPS, None, ALU.add))
                    v.sem_inc(root_in)
                    bstep(v.tensor_tensor(sc[:, 7, fo:fo + 1], mv[:, fo, 0:1], cur[:, 0, fo:fo + 1], ALU.add))
                    bstep(v.tensor_tensor(sc[:, 7, fo:fo + 1], cur[:, 0, fo:fo + 1], sc[:, 7, fo:fo + 1], ALU.subtract))
                    v.wait_ge(act_root, l * 4 + fo + 2)
                    bstep(v.reciprocal(sc[:, 2, 0:1], sc[:, 1, 0:1]))
                    bstep(v.scalar_tensor_tensor(out=sc[:, 5, 0:1], in0=sc[:, 0, 0:1], scalar=sc[:, 2, 0:1], in1=sc[:, 2, 0:1], op0=ALU.mult, op1=ALU.mult))
                    bstep(v.tensor_scalar(sc[:, 6, 0:1], sc[:, 5, 0:1], -0.5, 1.5, ALU.mult, ALU.add))
                    bstep(v.scalar_tensor_tensor(out=sc[:, 3, fo:fo + 1], in0=sc[:, 2, 0:1], scalar=sc[:, 6, 0:1], in1=cur[:, 1, fo:fo + 1], op0=ALU.mult, op1=ALU.mult))
                    bstep(v.scalar_tensor_tensor(out=sc[:, 4, fo:fo + 1], in0=sc[:, 7, fo:fo + 1], scalar=sc[:, 3, fo:fo + 1], in1=cur[:, 2, fo:fo + 1], op0=ALU.mult, op1=ALU.add))
                    v.sem_inc(shift_ready)
                return n0[0]

            def attention(j):
                if j < NT:
                    r = rows(j)
                    for m, (bank, shape, dst) in enumerate(((3, None, None), (4, None, None))):
                        v.wait_ge(qkv_done, 3 * j + m + 1)
                        pr = P if m == 0 else r
                        src = ps[bank][0:pr, :]
                        if m == 0 and r < P:
                            src = src.rearrange("p (c n) -> p c n", n=P)[:, :, 0:r]
                        tmp = mixtmp[0:pr, 0, :]
                        o = mix[0:pr, j, :] if m == 0 else mixtmp[0:pr, 1, :]
                        if m == 0 and r < P:
                            tmp = tmp.rearrange("p (c n) -> p c n", n=P)[:, :, 0:r]
                            o = o.rearrange("p (c n) -> p c n", n=P)[:, :, 0:r]
                        if m == 1 and j > 0:
                            v.wait_ge(kv_done, j)
                        v.tensor_scalar(tmp, src, 0.0, None, ALU.min).then_inc(mix_t, 1)
                        v.wait_ge(mix_exp, 2 * j + m + 1)
                        step(v.scalar_tensor_tensor(out=o, in0=src, scalar=0.0, in1=tmp, op0=ALU.max, op1=ALU.add))
                    v.wait_ge(qkv_done, 3 * j + 3)
                    step(v.tensor_tensor(mixtmp[0:r, 2, :], ps[5][0:r, :], bv_bc[0:r, :], ALU.add))
                    v.sem_inc(mix_kv_in)
                    v.wait_ge(kv_done, j + 1)
                    kvp = ps[6][:, :].rearrange("p (a e) -> p a e", e=P)
                    if j == 0:
                        step(v.tensor_copy(kvacc, kvp))
                        step(v.tensor_copy(ksum[:, :], ps[7][:, 0:KD]))
                    else:
                        step(v.tensor_tensor(kvacc, kvp, kvacc, ALU.add))
                        step(v.tensor_tensor(ksum[:, :], ps[7][:, 0:KD], ksum[:, :], ALU.add))
                    v.sem_inc(kv_taken)
                    if j == NT - 1:
                        step(v.memset(kvblk[:, :], 0.0))
                        step(v.memset(ksblk[:, :], 0.0))
                        for h in range(2):
                            q = slice(h * HD, (h + 1) * HD)
                            step(v.tensor_copy(kvblk[q, :].rearrange("p (a e) -> p a e", e=P)[:, :, q], kvacc[q, :, q]))
                            for a in range(KD):
                                step(v.tensor_scalar(ksblk[q, a * P + h * HD:a * P + (h + 1) * HD], ones[q, 0:HD], ksum[q, a:a + 1], None, ALU.mult))
                        v.sem_inc(kvblk_ready)
                else:
                    for t in OUT_TILES[j - NT]:
                        r = rows(t)
                        num, den = ps[3], ps[4]
                        cols = lambda ap: ap.rearrange("p (c n) -> p c n", n=P)[:, :, 0:r]
                        v.wait_ge(nd_done, t + 1)
                        step(v.reciprocal(cols(mixtmp[:, 3, :]), cols(den[:, :])))
                        step(v.tensor_tensor(cols(mix[:, t, :]), cols(num[:, :]), cols(mixtmp[:, 3, :]), ALU.mult))
                        v.sem_inc(att_ready)
                        v.wait_ge(proj_done, t + 1)
                        if t == 0:
                            v.wait_ge(bp_loaded, 16)
                        step(v.tensor_tensor(mix[0:r, t, :], ps[5][0:r, :], bp_bc[0:r, :], ALU.add))
                        v.wait_ge(xtile_loaded, 16 * (t + 1))
                        step(v.tensor_tensor(mix[0:r, t, :], mix[0:r, t, :], xtile[0:r, :], ALU.add))
                        v.sem_inc(mix_done)

            def stage_rows(l):
                v.wait_ge(be_loaded, l * 16 + 16)
                for t in range(NT):
                    r = rows(t)
                    v.wait_ge(rowT, (l - 1) * NT + t + 1)
                    v.wait_ge(table_stored[t % 2], (l * (NT // 2) + t // 2) * 16)
                    v.tensor_tensor(stage[0:r, t % 2, :], ps[t % 2][0:r, :], be_bc[0:r, :], ALU.add).then_inc(staged, 1)
                for k in range(KD):
                    ins = v.tensor_scalar(aggT[:, k, 0:N], xT[:, k, :], eps1[:, bass.ds(l, 1)], None, ALU.mult)
                    ins.then_inc(flushed, 1) if k == KD - 1 else None

            messages(0, attention)
            general(0)
            before = n[0]
            per = batch_norm(0, before)
            with v.Fori(1, L) as l:
                stage_rows(l)
                messages(l, None)
                general(l)
                batch_norm(l, before + l * per)
            n[0] = before + L * per

            for t in range(NT):
                r = rows(t)
                v.wait_ge(rowT, (L - 1) * NT + t + 1)
                v.tensor_tensor(mix[0:r, t, :], ps[t % 2][0:r, :], mix[0:r, t, :], ALU.add).then_inc(x2_ready, 1)
                v.wait_ge(x2_ready, t + 1)
                step(v.bn_stats(stats[0:r, t, :], mix[0:r, t, :]))
                step(v.bn_aggr(mv[0:r, t, :], stats[0:r, t, :]))
            root_of_var(mv[:, :, 1], NT, L * 4 + 2)
            for t in range(NT):
                r = rows(t)
                if t >= 2:
                    v.wait_ge(lnT, t - 1)
                v.tensor_scalar(stage[0:r, t % 2, :], mix[0:r, t, :], mv[0:r, t, 0:1], sc[0:r, 3, t:t + 1], ALU.subtract, ALU.mult).then_inc(staged, 1)
            v.wait_ge(b2_loaded, 48)
            v.wait_ge(logits_done, NT)
            lgp = ps[6][:, 0:NT * NE].rearrange("p (t e) -> p t e", e=NE)
            lgt = lambda a: lg[:, a, :, :]
            col = lambda a: sc[:, a, :].unsqueeze(2).to_broadcast([P, NT, NE])
            step(v.tensor_tensor(lg[:, 0, 0:NT - 1, :], lgp[:, 0:NT - 1, :], bs_bc[:, :].unsqueeze(1).to_broadcast([P, NT - 1, NE]), ALU.add))
            step(v.memset(lg[:, 0, NT - 1, :], 0.0))
            step(v.tensor_tensor(lg[0:LAST, 0, NT - 1, :], lgp[0:LAST, NT - 1, :], bs_bc[0:LAST, :], ALU.add))
            step(v.tensor_reduce(sc[:, 0, :], lgt(0), AX.X, ALU.max))
            step(v.tensor_tensor(lgt(0), lgt(0), col(0), ALU.subtract))
            v.sem_inc(l_exp_in)
            v.wait_ge(l_exp, 1)
            step(v.tensor_reduce(sc[:, 1, :], lgt(1), AX.X, ALU.add))
            step(v.reciprocal(sc[:, 2, :], sc[:, 1, :]))
            step(v.tensor_tensor(lgt(1), lgt(1), col(2), ALU.mult))
            step(v.tensor_reduce(sc[:, 3, :], lgt(1), AX.X, ALU.max))
            step(v.tensor_tensor(lgt(2), lgt(1), col(3), ALU.is_equal))
            step(v.tensor_scalar(sc[:, 4, 0:NE], iota[:, 0:NE], -1.0, float(NE), ALU.mult, ALU.add))
            step(v.tensor_tensor(lgt(2), lgt(2), sc[:, 4, 0:NE].unsqueeze(1).to_broadcast([P, NT, NE]), ALU.mult))
            step(v.tensor_reduce(sc[:, 5, :], lgt(2), AX.X, ALU.max))
            step(v.tensor_tensor(lgt(2), lgt(2), col(5), ALU.is_equal))
            step(v.tensor_tensor(lgt(3), lgt(2), col(3), ALU.mult))
            v.sem_inc(gate_ready)
            for t in range(NT):
                r = rows(t)
                v.wait_ge(gateT_done, t + 1)
                v.tensor_copy(gateT[:, t * P:t * P + r], ps[t % 2][0:NE, 0:r]).then_inc(gateT_out, 1)
            for t in range(NT):
                r = rows(t)
                v.wait_ge(gb_done, t + 1)
                v.tensor_tensor(mix[0:r, t, :], ps[t % 2][0:r, :], mix[0:r, t, :], ALU.add).then_inc(gb_taken, 1)
            for e in range(NE):
                for t in range(NT):
                    r = rows(t)
                    v.wait_ge(y_done, e * NT + t + 1)
                    if e == 0:
                        v.wait_ge(gb_taken, t + 1)
                    else:
                        v.wait_ge(y_taken, (e - 1) * NT + t + 1)
                    v.scalar_tensor_tensor(out=mix[0:r, t, :], in0=ps[t % 2][0:r, :], scalar=lg[0:r, 3, t, e:e + 1],
                                           in1=mix[0:r, t, :], op0=ALU.mult, op1=ALU.add).then_inc(y_taken, 1)

        @block.scalar
        def _(a):
            def root(s, src, dst):
                a.wait_ge(root_in, s)
                a.activation(dst, src, ACT.Sqrt).then_inc(act_root, 1)

            root(1, sc[:, 0, :], sc[:, 1, :])
            for t in range(NT):
                r = rows(t)
                a.wait_ge(prepT, t + 1)
                a.activation(xT[:, :, t * P:t * P + r], ps[6 + t % 2][:, :].rearrange("p (c n) -> p c n", n=P)[:, :, 0:r], ACT.Copy).then_inc(xnT_ready, 1)
            a.wait_ge(idxT_ready, 1)
            for k in range(3):
                a.activation(idx_slot[:, k, :], idxT[:, k, :], ACT.Copy).then_inc(idx_ready, 1)

            def relu(l, k, c, tiles=U):
                a.wait_ge(summed, l * NC + c + 1)
                a.wait_ge(parts_done, l * NC + c + 1)
                a.activation(message[:, k, 0:tiles, :], gathered[:, k, 0:tiles, :], ACT.Relu).then_inc(relu_done, 1)

            def parts_copy(l, c, b, groups=U):
                a.wait_ge(parts_done, l * NC + c + 4)
                a.wait_ge(window_done, l * NC + c + 1)
                q = slice(0, groups * WIN)
                a.activation(parts[q, b, :], ps[b][q, :], ACT.Copy).then_inc(parts_out, 1)

            def message_step(l, i, first=False):
                for kk in range(STEP):
                    c, k = i * STEP + kk, kk % 3
                    relu(l, k, c)
                    a.wait_ge(relu_done, l * NC + c + 1)
                    at = idxT[:, bass.ds(c + 3, 1), :].rearrange("p a u -> p (a u)")
                    a.activation(idx_slot[:, k, :], at, ACT.Copy).then_inc(idx_ready, 1)
                    if not (first and kk == 0):
                        parts_copy(l, c - 1, (kk + 1) % 2)

            def messages(l, beside):
                message_step(l, 0, first=True)
                if beside:
                    for i in range(ITER):
                        if i > 0:
                            message_step(l, i)
                        beside(i)
                else:
                    with a.Fori(1, ITER) as i:
                        message_step(l, i)
                relu(l, 0, FULL, tiles=1)
                a.wait_ge(relu_done, l * NC + NC)
                a.activation(idx_slot[:, 0, :], idxT[:, 0, :], ACT.Copy).then_inc(idx_ready, 1)
                parts_copy(l, FULL - 1, (FULL - 1) % 2)
                parts_copy(l, FULL, FULL % 2, groups=1)

            def general(l):
                left = a.value_load(left_i[0:1, 0:1], min_val=0, max_val=1)
                with a.If(left > 0):
                    with a.Fori(0, NC) as c:
                        a.wait_ge(idx_ready, l * NC + NC + 3)
                        a.activation(idx_slot[:, 0, :], idxT[:, bass.ds(c, 1), :].rearrange("p a u -> p (a u)"), ACT.Copy).then_inc(slow_idx, 1)
                        a.wait_ge(slow_sum, l * NC + c + 1)
                        a.activation(message[:, 0, :, :], gathered[:, 0, :, :], ACT.Relu).then_inc(slow_relu, 1)
                        a.wait_ge(slow_win, (l * NC + c + 1) * NW)
                    a.activation(idx_slot[:, 0, :], idxT[:, 0, :], ACT.Copy)

            def dense(l):
                for fo in range(KD):
                    root(l * 4 + fo + 2, sc[:, 0, 0:1], sc[:, 1, 0:1])
                    a.wait_ge(shift_ready, l * 4 + fo + 1)
                    for s, (lo, w) in enumerate(CUT):
                        a.activation(zT[:, fo, lo:lo + w], ps[2 + 3 * (fo % 2) + s][:, 0:w], ACT.Relu,
                                     bias=sc[:, 4, fo:fo + 1], scale=sc[:, 3, fo:fo + 1]).then_inc(z_ready, 1)
                for s, (lo, w) in enumerate(CUT):
                    for fo in range(KD):
                        g = s * KD + fo
                        a.wait_ge(mm2_done, l * 12 + g + 1)
                        a.activation(xT[:, fo, lo:lo + w], ps[2 + g % 6][:, 0:w], ACT.Relu, bias=cur[:, 3, fo:fo + 1]).then_inc(x_ready, 1)

            def attention(j):
                if j < NT:
                    r = rows(j)
                    for m in range(2):
                        pr = P if m == 0 else r
                        tmp = mixtmp[0:pr, 0, :]
                        if m == 0 and r < P:
                            tmp = tmp.rearrange("p (c n) -> p c n", n=P)[:, :, 0:r]
                        a.wait_ge(mix_t, 2 * j + m + 1)
                        a.activation(tmp, tmp, ACT.Exp).then_inc(mix_exp, 1)

            messages(0, attention)
            general(0)
            dense(0)
            with a.Fori(1, L) as l:
                messages(l, None)
                general(l)
                dense(l)

            root(L * 4 + 2, sc[:, 0, :], sc[:, 1, :])
            for t in range(NT):
                r = rows(t)
                a.wait_ge(lnT, t + 1)
                a.activation(zT[:, :, t * P:t * P + r], ps[2 + t % 2][:, :].rearrange("p (c n) -> p c n", n=P)[:, :, 0:r], ACT.Copy).then_inc(lnT_out, 1)
            a.wait_ge(l_exp_in, 1)
            a.activation(lg[:, 1, :, :], lg[:, 0, :, :], ACT.Exp).then_inc(l_exp, 1)
            for e in range(NE):
                if e >= 2:
                    a.wait_ge(y_done, (e - 1) * NT)
                for f in range(KF):
                    for s, (lo, w) in enumerate(CUT):
                        a.wait_ge(h_done, e * 6 + f * 3 + s + 1)
                        a.activation(hT[e % 2][:, f, lo:lo + w], ps[2 + f * 3 + s][:, 0:w], ACT.Gelu,
                                     bias=params[:, 4 * NPAR + e * KF + f:4 * NPAR + e * KF + f + 1]).then_inc(h_ready, 1)

        @block.tensor
        def _(pe):
            def mm(o, lhsT, rhs, start, stop):
                return nc.tensor.matmul(o, lhsT, rhs, start=start, stop=stop)

            for _ in range(3):
                pe.sem_inc(parts_done)
            for _ in range(2):
                pe.sem_inc(parts_out)
                pe.sem_inc(window_done)
            pe.wait_ge(ident_ready, 1)
            for t in range(NT):
                r = rows(t)
                pe.wait_ge(ln_ready, t + 1)
                if t >= 2:
                    pe.wait_ge(xnT_ready, t - 1)
                for c in range(KD):
                    ins = pe.transpose(ps[6 + t % 2][:, c * P:c * P + r], xrow[0:r, t, c * P:(c + 1) * P], ident[0:r, 0:r])
                ins.then_inc(prepT, 1)
            pe.wait_ge(edges_ready, 1)
            for m, row in enumerate((3, 2, 5, 6)):
                for u in range(U):
                    ins = pe.transpose(ps[m][:, u * NC:(u + 1) * NC], edge_rows[:, row, u * P:(u + 1) * P], ident[0:NC, 0:NC])
                ins.then_inc(edgeT, 1)
            pe.transpose(ps[4][0:1, 0:NC], edge_sc[:, 0:1], ident[0:NC, 0:NC])
            pe.transpose(ps[4][0:1, P:P + NC], edge_sc[:, 1:2], ident[0:NC, 0:NC])
            pe.wait_ge(small_loaded, 96)
            npar = 4 * NPAR + NE * KF
            pe.transpose(ps[5][:, 0:npar], params_row[:, :], ident[0:npar, 0:npar]).then_inc(edgeT, 1)
            pe.wait_ge(prep_done, 1)

            def group_sums(l, k, b, c, tiles=U):
                pe.wait_ge(relu_done, l * NC + c + 1)
                pe.wait_ge(parts_out, l * NC + c + 1)
                for u in range(tiles):
                    ins = mm(ps[b][u * WIN:(u + 1) * WIN, :], onehot[:, k, u, :],
                             message[:, k, u, :], True, True)
                ins.then_inc(parts_done, 1)

            def fold_groups(l, b, c, groups=U):
                pe.wait_ge(parts_out, l * NC + c + 3)
                pe.wait_ge(flushed, l * (NC + 1) + c + 3)
                q = slice(0, groups * WIN)
                for m in range(KD):
                    ins = mm(ps[2][:, m * WIN:(m + 1) * WIN], parts[q, b, m * P:(m + 1) * P], fold[q, :], True, True)
                ins.then_inc(window_done, 1)

            def message_step(l, i, first=False):
                for kk in range(STEP):
                    c = i * STEP + kk
                    group_sums(l, kk % 3, kk % 2, c)
                    if not (first and kk == 0):
                        fold_groups(l, (kk + 1) % 2, c - 1)

            def messages(l, before, after):
                if before:
                    for i in range(ITER):
                        before(i)
                        message_step(l, i, first=i == 0)
                        after(i)
                else:
                    message_step(l, 0, first=True)
                    with pe.Fori(1, ITER) as i:
                        message_step(l, i)
                group_sums(l, 0, FULL % 2, FULL, tiles=1)
                fold_groups(l, (FULL - 1) % 2, FULL - 1)
                fold_groups(l, FULL % 2, FULL, groups=1)

            def general(l):
                left = pe.value_load(left_i[0:1, 0:1], min_val=0, max_val=1)
                with pe.If(left > 0):
                    with pe.Fori(0, NC) as c:
                        pe.wait_ge(slow_relu, l * NC + c + 1)
                        pe.sem_inc(slow_go)
                        with pe.Fori(0, NW) as w:
                            pe.wait_ge(slow_oh, (l * NC + c) * NW + w + 1)
                            for q in range(KD):
                                for u in range(U):
                                    ins = mm(ps[0][:, q * WIN:(q + 1) * WIN], message[:, 0, u, q * P:(q + 1) * P], f_oh[:, u, :], u == 0, u == U - 1)
                            ins.then_inc(slow_win, 1)
                    pe.wait_ge(slow_add, (l + 1) * NC * (2 * NW + 1) + 1)

            def attention(j):
                if j < NT:
                    r = rows(j)
                    cols = slice(j * P, j * P + r)
                    if j == 0:
                        pe.wait_ge(mixw_loaded, 96)
                    if j > 0:
                        pe.wait_ge(mix_kv_in, j)
                    for c in range(KD):
                        for k in range(KD):
                            mm(ps[3][:, c * P:c * P + r], wq[:, k, c * P:(c + 1) * P], xT[:, k, cols], k == 0, False)
                        ins = mm(ps[3][:, c * P:c * P + r], q_bias[:, c * P:(c + 1) * P], ones[0:1, 0:r], False, True)
                    ins.then_inc(qkv_done, 1)
                    for k in range(KD):
                        mm(ps[4][0:r, :], xT[:, k, cols], wk[:, k, :], k == 0, False)
                    mm(ps[4][0:r, :], ones[0:1, 0:r], k_bias, False, True).then_inc(qkv_done, 1)
                    for k in range(KD):
                        ins = mm(ps[5][0:r, :], xT[:, k, cols], wv[:, k, :], k == 0, k == KD - 1)
                    ins.then_inc(qkv_done, 1)
                else:
                    if j == NT:
                        pe.wait_ge(kvblk_ready, 1)
                        pe.wait_ge(wp_loaded, 16)
                    for t in OUT_TILES[j - NT]:
                        r = rows(t)
                        if t > 0:
                            pe.wait_ge(mix_done, t)
                        for bank, blk in ((3, kvblk), (4, ksblk)):
                            for c in range(KD):
                                ins = mm(ps[bank][:, c * P:c * P + r], blk[:, c * P:(c + 1) * P], mix[:, t, c * P:c * P + r], True, True)
                        ins.then_inc(nd_done, 1)
                        pe.wait_ge(att_ready, t + 1)
                        for k in range(KD):
                            ins = mm(ps[5][0:r, :], mix[:, t, k * P:k * P + r], wp[:, k, :], k == 0, k == KD - 1)
                        ins.then_inc(proj_done, 1)

            def key_value(j):
                if j >= NT:
                    return
                r = rows(j)
                pe.wait_ge(mix_kv_in, j + 1)
                if j > 0:
                    pe.wait_ge(kv_taken, j)
                for c in range(KD):
                    mm(ps[6][:, c * P:(c + 1) * P], mixtmp[0:r, 1, c * P:(c + 1) * P], mixtmp[0:r, 2, c * P:(c + 1) * P], True, True)
                    ins = mm(ps[7][:, c:c + 1], mixtmp[0:r, 1, c * P:(c + 1) * P], ones[0:r, 0:1], True, True)
                ins.then_inc(kv_done, 1)

            def dense(l):
                pe.wait_ge(flushed, (l + 1) * (NC + 1) + 2)
                pe.wait_ge(w1_loaded, l * 16 + 16)
                for fo in range(KD):
                    if fo >= 2:
                        pe.wait_ge(z_ready, l * 12 + 3 * (fo - 1))
                    for k in range(KD):
                        for s, (lo, w) in enumerate(CUT):
                            ins = mm(ps[2 + 3 * (fo % 2) + s][:, 0:w], w1[:, k, fo * P:(fo + 1) * P], aggT[:, k, lo:lo + w], k == 0, k == KD - 1)
                    ins.then_inc(mm1_done, 1)
                pe.wait_ge(z_ready, (l + 1) * 12)
                pe.wait_ge(w2_loaded, l * 16 + 16)
                for s, (lo, w) in enumerate(CUT):
                    for fo in range(KD):
                        g = s * KD + fo
                        if g >= 6:
                            pe.wait_ge(x_ready, l * 12 + g - 5)
                        for k in range(KD):
                            ins = mm(ps[2 + g % 6][:, 0:w], w2[:, k, fo * P:(fo + 1) * P], zT[:, k, lo:lo + w], k == 0, k == KD - 1)
                        ins.then_inc(mm2_done, 1)
                    if s > 0:
                        rows_of(l, s - 1)
                rows_of(l, len(CUT) - 1)

            def rows_of(l, s):
                pe.wait_ge(x_ready, l * 12 + (s + 1) * KD)
                for t in TILES_OF_CUT[s]:
                    r = rows(t)
                    if t >= 2:
                        free_rows(l, t)
                    for c in range(KD):
                        ins = pe.transpose(ps[t % 2][0:r, c * P:(c + 1) * P], xT[:, c, t * P:t * P + r], ident[:, :])
                    ins.then_inc(rowT, 1)

            def free_rows(l, t):
                if last[0]:
                    pe.wait_ge(x2_ready, t - 1)
                else:
                    pe.wait_ge(staged, l * NT + t - 1)

            last = [False]
            messages(0, attention, key_value)
            general(0)
            dense(0)
            with pe.Fori(1, L - 1) as l:
                messages(l, None, None)
                general(l)
                dense(l)
            last[0] = True
            messages(L - 1, None, None)
            general(L - 1)
            dense(L - 1)

            pe.wait_ge(b2_loaded, 48)
            for t in range(NT):
                r = rows(t)
                pe.wait_ge(staged, (L - 1) * NT + t + 1)
                if t >= 2:
                    pe.wait_ge(lnT_out, t - 1)
                for c in range(KD):
                    ins = pe.transpose(ps[2 + t % 2][:, c * P:c * P + r], stage[0:r, t % 2, c * P:(c + 1) * P], ident[0:r, 0:r])
                ins.then_inc(lnT, 1)
            for t in range(NT):
                r = rows(t)
                pe.wait_ge(lnT_out, t + 1)
                for k in range(KD):
                    ins = mm(ps[6][0:r, t * NE:(t + 1) * NE], zT[:, k, t * P:t * P + r], ws[:, k, :], k == 0, k == KD - 1)
                ins.then_inc(logits_done, 1)

            def hidden(e):
                for f in range(KF):
                    for s, (lo, w) in enumerate(CUT):
                        if e > 0:
                            pe.wait_ge(h_ready, (e - 1) * 6 + f * 3 + s + 1)
                    for k in range(KD):
                        for s, (lo, w) in enumerate(CUT):
                            ins = mm(ps[2 + f * 3 + s][:, 0:w], ew1[:, e, k, f * P:(f + 1) * P], zT[:, k, lo:lo + w], k == 0, k == KD - 1)
                            if k == KD - 1:
                                ins.then_inc(h_done, 1)

            pe.wait_ge(ffn_loaded, 2 * NE * 16)
            pe.wait_ge(l_exp_in, 1)
            hidden(0)
            pe.wait_ge(gate_ready, 1)
            for t in range(NT):
                r = rows(t)
                if t >= 2:
                    pe.wait_ge(gateT_out, t - 1)
                pe.transpose(ps[t % 2][0:NE, 0:r], lg[0:r, 3, t, :], ident[0:r, 0:r]).then_inc(gateT_done, 1)
            for t in range(NT):
                r = rows(t)
                if t == 0:
                    pe.wait_ge(gateT_out, NT)
                if t >= 2:
                    pe.wait_ge(gb_taken, t - 1)
                mm(ps[t % 2][0:r, :], gateT[:, t * P:t * P + r], b2rows, True, True).then_inc(gb_done, 1)
            for e in range(NE):
                if e + 1 < NE:
                    hidden(e + 1)
                pe.wait_ge(h_ready, (e + 1) * 6)
                for t in range(NT):
                    r = rows(t)
                    if e == 0 and t < 2:
                        pe.wait_ge(gb_taken, NT)
                    else:
                        pe.wait_ge(y_taken, e * NT + t - 1)
                    for f in range(KF):
                        ins = mm(ps[t % 2][0:r, :], hT[e % 2][:, f, t * P:t * P + r], ew2[:, e, f, :], f == 0, f == KF - 1)
                    ins.then_inc(y_done, 1)


def kernel(**inputs):
    import numpy as _np
    import concourse.bacc as _bacc
    from concourse import mybir as _mybir
    from concourse.bass_utils import run_bass_kernel_spmd as _run

    nc = _bacc.Bacc("TRN2", target_bir_lowering=False, num_devices=1)
    arrays, io = {}, {}
    for name in inputs:
        a = _np.ascontiguousarray(inputs[name])
        arrays[f"in_{name}"] = a
        io[name] = nc.dram_tensor(f"in_{name}", a.shape, _mybir.dt.from_np(a.dtype), kind="ExternalInput").ap()
    shape = inputs["x"].shape
    out = nc.dram_tensor("out_0", shape, _mybir.dt.float32, kind="ExternalOutput").ap()
    build_gps_block(nc, io, out)
    r = _run(nc, [arrays], core_ids=[0])
    return r.results[0]["out_0"]
```

```python
import concourse.bass as bass
from concourse import mybir
from contextlib import ExitStack


def build_gps_block(nc, io, out):
    f32, i32 = mybir.dt.float32, mybir.dt.int32
    ALU, ACT, AX = mybir.AluOpType, mybir.ActivationFunctionType, mybir.AxisListType

    P = 128
    N, D = io["x"].shape
    E = io["src"].shape[0]
    L = io["L0_gnn_W1"].shape[0]
    NE, _, F = io["L0_ffn_W1"].shape
    HD = D // 8
    EPS = 1e-5
    KD = D // P
    KF = F // P
    NT = -(-N // P)
    LAST = N - (NT - 1) * P
    CUT = [(0, 512), (512, 512), (1024, N - 1024)]
    TILES_OF_CUT = [range(0, 4), range(4, 8), range(8, NT)]
    U = 6
    G = P // 32
    CE = U * P
    NC = -(-E // CE)
    FULL = E // CE
    TAIL = E - FULL * CE
    STEP = 4
    assert NC == FULL + 1 and 0 < TAIL <= P and FULL % STEP == 0
    ITER = FULL // STEP
    WIN = 32
    NW = -(-N // WIN)
    AW = N + WIN + 2
    FAR = 4000.0
    NS = (N + NE * (P - 1)) // P
    BIG = 8000.0
    QS = len(CUT) * KD
    pe_jobs = [[] for _ in range(2 * FULL)]
    act_jobs = [[] for _ in range(2 * FULL)]
    dve_jobs = [[] for _ in range(2 * FULL)]
    for i in range(QS):
        pe_jobs[i].append(("q", i))
        act_jobs[i + 1].append(("q", i))
        dve_jobs[i + 2].append(("q", i))
    KV0 = QS + 1
    for t in range(NT):
        at = KV0 + 3 * t
        pe_jobs[at].append(("k", t))
        pe_jobs[at + 1].append(("v", t))
        pe_jobs[at + 4].append(("kv", t))
        act_jobs[at + 1].append(("k", t))
        dve_jobs[at + 2] += [("k", t), ("v", t)]
    dve_jobs[KV0 + 3 * NT + 2].append(("blocks", 0))
    ATT0 = FULL + 1
    for i in range(QS):
        pe_jobs[ATT0 + 2 * i].append(("att", i))
        dve_jobs[ATT0 + 2 * i + 1].append(("att", i))
    PROJ0 = ATT0 + 2 * QS + 1
    for t in range(NT):
        pe_jobs[PROJ0 + 2 * t].append(("proj", t))
        dve_jobs[PROJ0 + 2 * t + 1].append(("proj", t))

    def rows(t):
        return LAST if t == NT - 1 else P

    with ExitStack() as ctx:
        def sb(name, shape, dt=f32):
            return ctx.enter_context(nc.sbuf_tensor(name, shape, dt))

        def sem(name):
            return ctx.enter_context(nc.semaphore(name))

        table = nc.dram_tensor("x_table", [N, D], f32).ap()
        y_table = nc.dram_tensor("y_table", [NS * P, D], f32).ap()

        ring = sb("ring", [P, STEP * U * D])
        slots = ring[:, :].rearrange("p (k u d) -> p k u d", k=STEP, u=U)
        xrow = ring[:, 0:NT * D].rearrange("p (t d) -> p t d", t=NT)
        xplus = ring[:, NT * D:2 * NT * D].rearrange("p (t d) -> p t d", t=NT)
        ew1 = ring[:, 0:NE * KD * F].rearrange("p (e k f) -> p e k f", e=NE, k=KD)
        ew2 = sb("ew2", [P, NE, KF, D])
        onehot = sb("onehot", [P, STEP, U, WIN])
        aggT = sb("aggT", [P, KD, AW])
        xT = sb("xT", [P, KD, NT * P])
        aggflat = aggT[:, :, :].rearrange("p k n -> p (k n)")
        xg = [aggflat[:, b * D:(b + 1) * D] for b in range(4)]
        xgT = [aggflat[:, (4 + b) * D:(5 + b) * D] for b in range(2)]
        hid = [aggflat[:, 6 * D + b * F:6 * D + (b + 1) * F] for b in range(2)]
        hidT = [aggflat[:, 6 * D + (2 + b) * F:6 * D + (3 + b) * F] for b in range(2)]
        yrow = [aggflat[:, 6 * D + 4 * F + b * D:6 * D + 4 * F + (b + 1) * D] for b in range(2)]
        b2_bc = xT[:, :, :].rearrange("p k n -> p (k n)")[:, 0:NE * D].rearrange("p (e d) -> p e d", e=NE)
        zT = sb("zT", [P, KD, N])
        zflat = zT[:, :, :].rearrange("p k n -> p (k n)")
        wq = zflat[:, 0:KD * D].rearrange("p (k n) -> p k n", k=KD)
        wk = zflat[:, KD * D:2 * KD * D].rearrange("p (k n) -> p k n", k=KD)
        wp = wq
        place_oh = zflat[:, 0:NT * P].rearrange("p (t n) -> p t n", t=NT)
        tile_oh = zflat[:, NT * P:NT * (P + NS)].rearrange("p (t n) -> p t n", t=NT)
        compared = zflat[:, NT * (P + NS):]
        bv_bc = zflat[:, 2 * KD * D:2 * KD * D + D]
        w1 = sb("w1", [P, KD, D])
        w1flat = w1[:, :, :].rearrange("p k n -> p (k n)")
        att_exp = [w1flat[:, b * D:(b + 1) * D] for b in range(2)]
        k_rows = w1flat[:, D:2 * D]
        v_rows = w1flat[:, 2 * D:2 * D + KD * (P + 1)].rearrange("p (c n) -> p c n", c=KD)
        w2 = sb("w2", [P, KD, D])
        wv = w2
        b1_bc = w1[:, :, :].rearrange("p k n -> p (k n)").rearrange("p (e f) -> p e f", e=NE)
        mix = sb("mix", [P, NT, D])
        edge_rows = mix[0:NC, :, :].rearrange("p t d -> p (t d)")[:, 0:6 * CE].rearrange("p (a e) -> p a e", a=6)
        we_bc = sb("we_bc", [P, D])
        be_bc = sb("be_bc", [P, D])
        bp_bc = be_bc
        stage = sb("stage", [P, 2, D])
        xtile = stage[:, 1, :]
        kvblk = sb("kvblk", [P, D])
        ksblk = sb("ksblk", [P, D])
        k_bias = ksblk[0:1, :]
        parts = sb("parts", [P, 2, D])
        fold = sb("fold", [P, WIN])
        idxT = sb("idxT", [P, NC + STEP - 1, U], i32)
        wT = sb("wT", [P, NC, U])
        remT = sb("remT", [P, NC, U])
        relT = sb("relT", [P, NC, U])
        idx_slot = sb("idx_slot", [P, STEP, U], i32)
        base_i = sb("base_i", [1, NC], i32)
        left_f = sb("left_f", [1, NC + 1])
        left_i = sb("left_i", [1, 1], i32)
        ident = sb("ident", [P, P])
        iota_i = sb("iota_i", [P, WIN], i32)
        iota = sb("iota", [P, WIN])
        ones = sb("ones", [P, P])
        NPAR = L * KD
        ALLPAR = 4 * NPAR + NE * KF + KD
        params_row = sb("params_row", [ALLPAR, P])
        params = sb("params", [P, ALLPAR])
        bq_neg = sb("bq_neg", [P, KD])
        bq_one = sb("bq_one", [P, KD])
        par = params[:, 0:4 * L * KD].rearrange("p (a q) -> p a q", a=4)
        cur = sb("cur", [P, 4, KD])
        eps_bc = sb("eps_bc", [P, L])
        eps1 = sb("eps1", [P, L])
        stats = sb("stats", [P, NT, 6])
        mv = sb("mv", [P, NT, 2])
        sc = sb("sc", [P, 8, NT])
        edge_sc = sb("edge_sc", [NC, 4])
        ksum = sb("ksum", [P, KD])
        f_oh = sb("f_oh", [P, U, WIN])
        f_rem = sb("f_rem", [P, U])
        ws = sb("ws", [P, KD, NE])
        bs_bc = sb("bs_bc", [P, NE])
        lg = sb("lg", [P, 4, NT, NE])
        ln_rows = [ring[:, NE * KD * F + t * D:NE * KD * F + (t + 1) * D] for t in range(NT - 2)] + [stage[:, t, :] for t in range(2)]
        tri = sb("tri", [P, P])
        count_i = sb("count_i", [P, P], i32)
        count = sb("count", [P, P])
        token = sb("token", [P, NT])
        valid = sb("valid", [P, NT])
        experts = sb("experts", [P, 4, NE])
        rank_of = sb("rank_of", [P, NS])
        expert_i = sb("expert_i", [1, NS], i32)
        slot_i = sb("slot_i", [P, NT], i32)
        token_i = sb("token_i", [P, NS], i32)

        ps = [ctx.enter_context(nc.psum_tensor(f"ps{i}", [P, 512], f32)) for i in range(8)]

        ident_ready = sem("ident_ready")
        iota_made = sem("iota_made")
        pads_ready = sem("pads_ready")
        x_loaded = sem("x_loaded")
        edges_loaded = sem("edges_loaded")
        small_loaded = sem("small_loaded")
        mixw_loaded = sem("mixw_loaded")
        wp_loaded = sem("wp_loaded")
        xtile_loaded = sem("xtile_loaded")
        we_loaded = sem("we_loaded")
        be_loaded = sem("be_loaded")
        bp_loaded = sem("bp_loaded")
        w1_loaded = sem("w1_loaded")
        w2_loaded = sem("w2_loaded")
        ffn_loaded = sem("ffn_loaded")
        router_loaded = sem("router_loaded")
        table_stored = [sem(f"table_stored{b}") for b in range(2)]
        out_stored = sem("out_stored")
        dve = sem("dve_steps")
        act_root = sem("act_root")
        root_in = sem("root_in")
        ln_ready = sem("ln_ready")
        xp_ready = sem("xp_ready")
        prepT = sem("prepT")
        xnT_ready = sem("xnT_ready")
        src_ready = sem("src_ready")
        edges_ready = sem("edges_ready")
        edgeT = sem("edgeT")
        idxT_ready = sem("idxT_ready")
        prep_done = sem("prep_done")
        idx_ready = sem("idx_ready")
        gather_go = sem("gather_go")
        got = [sem(f"got{k}") for k in range(STEP)]
        summed = sem("summed")
        relu_done = sem("relu_done")
        parts_done = sem("parts_done")
        parts_out = sem("parts_out")
        window_done = sem("window_done")
        flushed = sem("flushed")
        slow_idx = sem("slow_idx")
        slow_got = sem("slow_got")
        slow_sum = sem("slow_sum")
        slow_relu = sem("slow_relu")
        slow_oh = sem("slow_oh")
        slow_win = sem("slow_win")
        slow_add = sem("slow_add")
        slow_go = sem("slow_go")
        stats_ready = sem("stats_ready")
        q_done = sem("q_done")
        k_done = sem("k_done")
        v_done = sem("v_done")
        mix_t = sem("mix_t")
        mix_exp = sem("mix_exp")
        q_ready = sem("q_ready")
        k_ready = sem("k_ready")
        v_ready = sem("v_ready")
        kv_done = sem("kv_done")
        kvblk_ready = sem("kvblk_ready")
        nd_done = sem("nd_done")
        att_ready = sem("att_ready")
        proj_done = sem("proj_done")
        mix_done = sem("mix_done")
        mm1_done = sem("mm1_done")
        shift_ready = sem("shift_ready")
        z_ready = sem("z_ready")
        mm2_done = sem("mm2_done")
        x_ready = sem("x_ready")
        rowT = sem("rowT")
        staged = sem("staged")
        x2_ready = sem("x2_ready")
        lnT = sem("lnT")
        lnT_out = sem("lnT_out")
        logits_done = sem("logits_done")
        l_exp_in = sem("l_exp_in")
        l_exp = sem("l_exp")
        gate_ready = sem("gate_ready")
        consts_made = sem("consts_made")
        ffn_bias_loaded = sem("ffn_bias_loaded")
        rows_stored = sem("rows_stored")
        rank_done = sem("rank_done")
        places_ready = sem("places_ready")
        token_done = sem("token_done")
        token_ready = sem("token_ready")
        xg_got = [sem(f"xg_got{b}") for b in range(4)]
        xgT_done = sem("xgT_done")
        xgT_ready = sem("xgT_ready")
        hid_done = sem("hid_done")
        hid_sum = sem("hid_sum")
        hid_ready = sem("hid_ready")
        hidT_done = sem("hidT_done")
        hidT_ready = sem("hidT_ready")
        y_done = sem("y_done")
        y_out = sem("y_out")
        y_stored = [sem(f"y_stored{b}") for b in range(2)]
        yg_got = [sem(f"yg_got{t}") for t in range(NT)]
        res_ready = sem("res_ready")

        block = ctx.enter_context(nc.Block())

        def by_tile(ap):
            return ap.rearrange("p (t n) -> p t n", n=P)

        def nd_banks(i):
            return (ps[3], ps[4]) if i % 2 == 0 else (ps[6], ps[7])

        @block.sync
        def _(sp):
            sp.wait_ge(pads_ready, 1)
            sp.dma_start(xrow[:, 0:NT - 1, :], io["x"][0:(NT - 1) * P, :].rearrange("(t p) d -> p t d", p=P)).then_inc(x_loaded, 16)
            sp.dma_start(xrow[0:LAST, NT - 1, :], io["x"][(NT - 1) * P:N, :]).then_inc(x_loaded, 16)
            sp.wait_ge(pads_ready, 4)
            for j, name in ((0, "src"), (1, "dst"), (2, "edge_weight1")):
                flat = io[name] if name != "edge_weight1" else io[name].rearrange("e a -> (e a)")
                dst = edge_rows[:, j, :] if name == "edge_weight1" else edge_rows[:, j, :].bitcast(i32)
                sp.dma_start(dst[0:FULL, :], flat[0:FULL * CE].rearrange("(c e) -> c e", e=CE)).then_inc(edges_loaded, 16)
                sp.dma_start(dst[FULL:NC, 0:TAIL], flat[FULL * CE:E].rearrange("(c e) -> c e", c=1)).then_inc(edges_loaded, 16)
            for a, name in enumerate(("b1", "gamma", "beta", "b2")):
                sp.dma_start(params_row[a * NPAR:(a + 1) * NPAR, :],
                             io["L0_gnn_" + name].rearrange("l (c p) -> (l c) p", p=P)).then_inc(small_loaded, 16)
            sp.dma_start(params_row[4 * NPAR:ALLPAR - KD, :], io["L0_ffn_b1"].rearrange("e (c p) -> (e c) p", p=P)).then_inc(small_loaded, 16)
            sp.dma_start(params_row[ALLPAR - KD:, :], io["L0_mix_bq"].rearrange("(c p) -> c p", p=P)).then_inc(small_loaded, 16)
            sp.dma_start(eps_bc[:, :], io["L0_gnn_eps"].rearrange("(a l) -> a l", a=1).to_broadcast([P, L])).then_inc(small_loaded, 16)
            sp.dma_start(be_bc[:, :], io["L0_gnn_be"][0:1, :].to_broadcast([P, D])).then_inc(be_loaded, 16)
            sp.dma_start(we_bc[:, :], io["L0_gnn_We"][0, :, :].to_broadcast([P, D])).then_inc(we_loaded, 16)
            sp.dma_start(wq, io["L0_mix_Wq"].rearrange("(k p) n -> p k n", p=P)).then_inc(mixw_loaded, 16)
            sp.dma_start(wk, io["L0_mix_Wk"].rearrange("(k p) n -> p k n", p=P)).then_inc(mixw_loaded, 16)
            sp.dma_start(wv[:, :, :], io["L0_mix_Wv"].rearrange("(k p) n -> p k n", p=P)).then_inc(mixw_loaded, 16)
            sp.dma_start(k_bias, io["L0_mix_bk"].rearrange("(a n) -> a n", a=1)).then_inc(mixw_loaded, 16)
            sp.dma_start(bv_bc, io["L0_mix_bv"].rearrange("(a n) -> a n", a=1).to_broadcast([P, D])).then_inc(mixw_loaded, 16)
            for t in range(NT):
                sp.wait_ge(xp_ready, t + 1)
                sp.dma_start(table[t * P:t * P + rows(t), :], xplus[0:rows(t), t, :]).then_inc(table_stored[t % 2], 16)
            sp.wait_ge(v_done, NT)
            sp.dma_start(w2[:, :, :], io["L0_gnn_W2"][0].rearrange("(k p) n -> p k n", p=P)).then_inc(w2_loaded, 16)
            sp.wait_ge(kv_done, NT)
            sp.dma_start(w1[:, :, :], io["L0_gnn_W1"][0].rearrange("(k p) n -> p k n", p=P)).then_inc(w1_loaded, 16)

            def edge_terms(l):
                sp.wait_ge(mm1_done, l * KD)
                sp.dma_start(we_bc[:, :], io["L0_gnn_We"].rearrange("l a d -> (l a) d")[bass.ds(l, 1), :].to_broadcast([P, D])).then_inc(we_loaded, 16)
                sp.dma_start(be_bc[:, :], io["L0_gnn_be"][bass.ds(l, 1), :].to_broadcast([P, D])).then_inc(be_loaded, 16)

            def first_weights(l):
                sp.dma_start(w1[:, :, :], io["L0_gnn_W1"].rearrange("l (k p) n -> p (l k) n", p=P)[:, bass.ds(l * KD, KD), :]).then_inc(w1_loaded, 16)

            def store_table(l):
                for t in range(NT):
                    sp.wait_ge(staged, (l - 1) * NT + t + 1)
                    sp.dma_start(table[t * P:t * P + rows(t), :], xplus[0:rows(t), t, :]).then_inc(table_stored[t % 2], 16)

            def second_weights(l):
                sp.wait_ge(mm2_done, l * 12)
                sp.dma_start(w2[:, :, :], io["L0_gnn_W2"].rearrange("l (k p) n -> p (l k) n", p=P)[:, bass.ds(l * KD, KD), :]).then_inc(w2_loaded, 16)

            edge_terms(1)
            store_table(1)
            second_weights(1)
            sp.dma_start(wp, io["L0_mix_Wp"].rearrange("(k p) n -> p k n", p=P)).then_inc(wp_loaded, 16)
            sp.dma_start(bp_bc[:, :], io["L0_mix_bp"].rearrange("(a n) -> a n", a=1).to_broadcast([P, D])).then_inc(bp_loaded, 16)
            for t in range(NT):
                if t > 0:
                    sp.wait_ge(mix_done, t)
                sp.dma_start(xtile[0:rows(t), :], io["x"][t * P:t * P + rows(t), :]).then_inc(xtile_loaded, 16)
            sp.wait_ge(mix_done, NT)
            first_weights(1)
            with sp.Fori(2, L) as l:
                edge_terms(l)
                first_weights(l)
                store_table(l)
                second_weights(l)
            sp.wait_ge(mm1_done, (L - 1) * 4 + 1)
            for e in range(NE):
                sp.dma_start(ew1[:, e, :, :], io["L0_ffn_W1"][e].rearrange("(k p) f -> p k f", p=P)).then_inc(ffn_loaded, 16)
                sp.dma_start(ew2[:, e, :, :], io["L0_ffn_W2"][e].rearrange("(k p) f -> p k f", p=P)).then_inc(ffn_loaded, 16)
            sp.dma_start(ws[:, :, :], io["L0_ffn_Ws"].rearrange("(k p) e -> p k e", p=P)).then_inc(router_loaded, 16)
            sp.dma_start(bs_bc[:, :], io["L0_ffn_bs"].rearrange("(a e) -> a e", a=1).to_broadcast([P, NE])).then_inc(router_loaded, 16)
            sp.wait_ge(mm1_done, L * KD)
            sp.dma_start(b1_bc, io["L0_ffn_b1"].rearrange("(a e) f -> a e f", a=1).to_broadcast([P, NE, F])).then_inc(ffn_bias_loaded, 16)
            for t in range(NT):
                sp.wait_ge(staged, (L - 1) * NT + t + 1)
                sp.dma_start(table[t * P:t * P + rows(t), :], ln_rows[t][0:rows(t), :]).then_inc(rows_stored, 16)
            sp.wait_ge(x2_ready, NT)
            sp.dma_start(b2_bc, io["L0_ffn_b2"].rearrange("(a e) d -> a e d", a=1).to_broadcast([P, NE, D])).then_inc(ffn_bias_loaded, 16)
            for j in range(NS):
                sp.wait_ge(y_out, j + 1)
                sp.dma_start(y_table[j * P:(j + 1) * P, :], yrow[j % 2]).then_inc(y_stored[j % 2], 16)
            for t in range(NT):
                sp.wait_ge(res_ready, t + 1)
                sp.dma_start(out[t * P:t * P + rows(t), :], mix[0:rows(t), t, :]).then_inc(out_stored, 16)
            sp.wait_ge(out_stored, NT * 16)

        @block.gpsimd
        def _(gp):
            gp.memset(xrow[:, NT - 1, :], 0.0).then_inc(pads_ready, 1)
            gp.memset(edge_rows[:, 0, :], 0.0).then_inc(pads_ready, 1)
            gp.memset(edge_rows[:, 1, :].bitcast(i32), int(FAR)).then_inc(pads_ready, 1)
            gp.memset(edge_rows[:, 2, :], 0.0).then_inc(pads_ready, 1)
            gp.memset(ident[:, :], 0.0).then_inc(iota_made, 1)
            gp.memset(ones[:, :], 1.0).then_inc(iota_made, 1)
            gp.iota(iota_i[:, :], [[1, WIN]], base=0, channel_multiplier=0).then_inc(iota_made, 1)
            gp.wait_ge(iota_made, 3)
            gp.memset(fold[:, :], 0.0).then_inc(iota_made, 1)
            for g in range(G):
                gp.wait_ge(iota_made, 4 + g)
                gp.affine_select(out=fold[:, :], in_=fold[:, :], compare_op=ALU.not_equal, fill=1.0, base=-WIN * g,
                                 pattern=[[-1, WIN]], channel_multiplier=1).then_inc(iota_made, 1)
            gp.affine_select(out=ident[:, :], in_=ident[:, :], compare_op=ALU.not_equal, fill=1.0, base=0,
                             pattern=[[-1, P]], channel_multiplier=1).then_inc(ident_ready, 1)

            def gather(k, u, done):
                gp.indirect_dma_start(out=slots[:, k, u, :], out_offset=None, in_=table[:, :],
                                      in_offset=bass.IndirectOffsetOnAxis(ap=idx_slot[:, k, u:u + 1], axis=0)
                                      ).then_inc(done, 16)

            def messages(l):
                for b in range(2):
                    gp.wait_ge(table_stored[b], (l + 1) * (NT // 2) * 16)
                gp.wait_ge(idx_ready, l * NC + STEP)
                gp.sem_inc(gather_go)
                with gp.Fori(0, ITER) as i:
                    for kk in range(STEP):
                        gp.wait_ge(idx_ready, l * NC + i * STEP + kk + 1)
                        gp.wait_ge(parts_done, l * NC + i * STEP + kk + 1)
                        gp.sem_inc(gather_go)
                        for u in range(U):
                            gather(kk, u, got[kk])
                gp.wait_ge(idx_ready, l * NC + FULL + 1)
                gp.wait_ge(parts_done, l * NC + FULL + 1)
                gp.sem_inc(gather_go)
                gather(0, 0, got[0])
                gp.wait_ge(prep_done, 1)
                left = gp.value_load(left_i[0:1, 0:1], min_val=0, max_val=1)
                with gp.If(left > 0):
                    with gp.Fori(0, NC) as c:
                        gp.wait_ge(slow_idx, l * NC + c + 1)
                        gp.sem_inc(gather_go)
                        for u in range(U):
                            gather(0, u, slow_got)

            gp.iota(count_i[:, :], [[1, P]], base=0, channel_multiplier=0).then_inc(consts_made, 1)
            gp.iota(token_i[:, 0:NT], [[P, NT]], base=0, channel_multiplier=1).then_inc(consts_made, 1)
            gp.memset(tri[:, :], 1.0).then_inc(consts_made, 1)
            gp.memset(valid[:, :], 1.0).then_inc(consts_made, 1)
            gp.wait_ge(consts_made, 4)
            gp.affine_select(out=tri[:, :], in_=tri[:, :], compare_op=ALU.is_gt, fill=0.0, base=0,
                             pattern=[[1, P]], channel_multiplier=-1).then_inc(consts_made, 1)
            gp.affine_select(out=valid[:, NT - 1:NT], in_=valid[:, NT - 1:NT], compare_op=ALU.is_gt, fill=0.0, base=LAST,
                             pattern=[[0, 1]], channel_multiplier=-1).then_inc(consts_made, 1)
            gp.wait_ge(be_loaded, 16)
            for t in range(NT):
                gp.wait_ge(ln_ready, t + 1)
                gp.tensor_tensor(xplus[:, t, :], xrow[:, t, :], be_bc[:, :], ALU.add).then_inc(xp_ready, 1)
            gp.wait_ge(xp_ready, NT)
            gp.wait_ge(prepT, NT)
            gp.sem_inc(gather_go)
            messages(0)
            with gp.Fori(1, L) as l:
                messages(l)

            def gather_rows(dst, src, idx, done):
                gp.indirect_dma_start(out=dst, out_offset=None, in_=src,
                                      in_offset=bass.IndirectOffsetOnAxis(ap=idx, axis=0)).then_inc(done, 16)

            gp.wait_ge(token_ready, 1)
            gp.wait_ge(rows_stored, NT * 16)
            for j in range(NS):
                if j >= 4:
                    gp.wait_ge(xgT_done, j - 3)
                gather_rows(xg[j % 4], table[:, :], token_i[:, j:j + 1], xg_got[j % 4])
            for b in range(2):
                gp.wait_ge(y_stored[b], (NS + 1 - b) // 2 * 16)
            for t in range(NT):
                gather_rows(ln_rows[t], y_table[:, :], slot_i[:, t:t + 1], yg_got[t])

        @block.vector
        def _(v):
            n = [0]

            def step(ins):
                ins.then_inc(dve, 1)
                n[0] += 1
                v.wait_ge(dve, n[0])

            def chunked(m):
                return ps[m][:, 0:U * NC].rearrange("p (u c) -> p c u", u=U)

            def root_of_var(mvv, cnt, s):
                step(v.tensor_scalar(sc[:, 0, 0:cnt], mvv, EPS, None, ALU.add))
                v.sem_inc(root_in)
                v.wait_ge(act_root, s)
                step(v.reciprocal(sc[:, 2, 0:cnt], sc[:, 1, 0:cnt]))
                step(v.tensor_tensor(sc[:, 4, 0:cnt], sc[:, 0, 0:cnt], sc[:, 2, 0:cnt], ALU.mult))
                step(v.tensor_tensor(sc[:, 5, 0:cnt], sc[:, 4, 0:cnt], sc[:, 2, 0:cnt], ALU.mult))
                step(v.tensor_scalar(sc[:, 6, 0:cnt], sc[:, 5, 0:cnt], -0.5, 1.5, ALU.mult, ALU.add))
                step(v.tensor_tensor(sc[:, 3, 0:cnt], sc[:, 2, 0:cnt], sc[:, 6, 0:cnt], ALU.mult))

            v.wait_ge(edges_loaded, 96)
            step(v.tensor_copy(edge_rows[:, 3, :], edge_rows[:, 0, :].bitcast(i32)))
            v.sem_inc(src_ready)
            v.wait_ge(x_loaded, 32)
            for t in range(NT):
                ins = v.bn_stats(stats[:, t, :], xrow[:, t, :])
            step(ins)
            for t in range(NT):
                ins = v.bn_aggr(mv[:, t, :], stats[:, t, :])
            step(ins)
            root_of_var(mv[:, :, 1], NT, 1)
            for t in range(NT):
                v.tensor_scalar(xrow[:, t, :], xrow[:, t, :], mv[:, t, 0:1], sc[:, 3, t:t + 1], ALU.subtract, ALU.mult).then_inc(ln_ready, 1)
                if t == 1:
                    v.wait_ge(edgeT, 1)
                    step(v.tensor_copy(idxT[:, 0:NC, :], chunked(0)))
                    step(v.tensor_copy(idxT[:, NC:NC + STEP - 1, :], idxT[:, 1:STEP, :]))
                    v.sem_inc(idxT_ready)

            step(v.tensor_copy(edge_rows[:, 4, :], edge_rows[:, 1, :].bitcast(i32)))
            step(v.tensor_reduce(edge_sc[:, 0:1], edge_rows[:, 4, :], AX.X, ALU.min))
            step(v.tensor_scalar(edge_rows[:, 5, :], edge_rows[:, 4, :], edge_sc[:, 0:1], None, ALU.subtract))
            step(v.tensor_scalar(edge_rows[:, 0, :], edge_rows[:, 5, :], float(WIN), BIG, ALU.is_lt, ALU.mult))
            step(v.tensor_tensor(edge_rows[:, 0, :], edge_rows[:, 0, :], edge_rows[:, 4, :], ALU.add))
            step(v.tensor_reduce(edge_sc[:, 1:2], edge_rows[:, 0, :], AX.X, ALU.min))
            v.sem_inc(edges_ready)
            v.wait_ge(iota_made, 3)
            v.tensor_copy(iota[:, :], iota_i[:, :])
            v.wait_ge(consts_made, 6)
            v.tensor_copy(count[:, :], count_i[:, :])
            step(v.tensor_copy(token[:, :], token_i[:, 0:NT]))
            v.tensor_tensor(token[:, :], token[:, :], valid[:, :], ALU.mult)
            v.memset(aggT[:, :, N:AW], 0.0)
            v.memset(xT[:, :, N:], 0.0)
            v.wait_ge(small_loaded, 112)
            step(v.tensor_scalar(eps1[:, :], eps_bc[:, :], 1.0, None, ALU.add))
            v.wait_ge(xnT_ready, NT)
            for k in range(KD):
                v.tensor_scalar(aggT[:, k, 0:N], xT[:, k, 0:N], eps1[:, 0:1], None, ALU.mult)

            v.wait_ge(edgeT, 4)
            v.tensor_copy(wT[:, :, :], chunked(1))
            v.tensor_copy(relT[:, :, :], chunked(2))
            v.tensor_copy(remT[:, :, :], chunked(3))
            v.wait_ge(edgeT, 5)
            v.tensor_copy(base_i[:, :], ps[4][0:1, 0:NC])
            v.tensor_copy(params[:, :], ps[5][:, 0:ALLPAR])
            step(v.tensor_copy(left_f[:, 0:NC], ps[4][0:1, P:P + NC]))
            step(v.tensor_reduce(left_f[:, NC:NC + 1], left_f[:, 0:NC], AX.X, ALU.min))
            step(v.tensor_scalar(left_i[:, :], left_f[:, NC:NC + 1], FAR, None, ALU.is_lt))
            v.tensor_scalar(bq_neg[:, :], params[:, ALLPAR - KD:], -1.0, None, ALU.mult)
            step(v.tensor_scalar(bq_one[:, :], params[:, ALLPAR - KD:], 1.0, None, ALU.add))
            v.sem_inc(flushed)
            v.sem_inc(flushed)
            v.sem_inc(flushed)
            v.sem_inc(slow_add)
            v.sem_inc(prep_done)

            def add_edges(l, k, c, uses, tiles=U):
                v.wait_ge(parts_done, l * NC + c + 1)
                v.tensor_tensor(onehot[:, k, :, :], iota[:, :].unsqueeze(1).to_broadcast([P, U, WIN]),
                                relT[:, bass.ds(c, 1), :].rearrange("p a u -> p (a u)").unsqueeze(2).to_broadcast([P, U, WIN]), ALU.is_equal)
                v.wait_ge(got[k], uses)
                for u in range(tiles):
                    ins = v.scalar_tensor_tensor(out=slots[:, k, u, :], in0=we_bc[:, :], scalar=wT[:, bass.ds(c, 1), u:u + 1].rearrange("p a b -> p (a b)"),
                                                 in1=slots[:, k, u, :], op0=ALU.mult, op1=ALU.add)
                ins.then_inc(summed, 1)

            def flush(l, c):
                base = v.value_load(base_i[0:1, bass.ds(c, 1)], min_val=0, max_val=N - 1)
                v.wait_ge(window_done, l * NC + c + 3)
                v.wait_ge(flushed, l * (NC + 1) + 3 + c)
                at = aggT[:, :, bass.ds(base, WIN)]
                v.tensor_tensor(at, ps[2][:, 0:P].rearrange("p (a b) -> p a b", a=KD), at, ALU.add).then_inc(flushed, 1)

            GOT = ITER * U * 16
            GOT0 = GOT + 16

            def message_step(l, i, first=False, beside=None):
                for kk in range(STEP):
                    add_edges(l, kk, i * STEP + kk, l * (GOT0 if kk == 0 else GOT) + (i + 1) * (U * 16))
                    if not (first and kk < 3):
                        flush(l, i * STEP + kk - 3)
                    if beside:
                        beside(l * FULL + i * STEP + kk)

            def messages(l, beside):
                v.wait_ge(we_loaded, l * 16 + 16)
                if beside:
                    for i in range(ITER):
                        message_step(l, i, first=i == 0, beside=beside)
                else:
                    message_step(l, 0, first=True)
                    with v.Fori(1, ITER) as i:
                        message_step(l, i)
                add_edges(l, 0, FULL, (l + 1) * GOT0, tiles=1)
                for c in range(FULL - 3, NC):
                    flush(l, c)

            def general(l):
                left = v.value_load(left_i[0:1, 0:1], min_val=0, max_val=1)
                with v.If(left > 0):
                    with v.Fori(0, NC) as c:
                        v.wait_ge(slow_got, (l * NC + c + 1) * U * 16)
                        for u in range(U):
                            ins = v.scalar_tensor_tensor(out=slots[:, 0, u, :], in0=we_bc[:, :], scalar=wT[:, bass.ds(c, 1), u:u + 1].rearrange("p a b -> p (a b)"),
                                                         in1=slots[:, 0, u, :], op0=ALU.mult, op1=ALU.add)
                        ins.then_inc(slow_sum, 1)
                        v.wait_ge(slow_add, (l * NC + c) * (2 * NW + 1) + 1)
                        v.tensor_copy(f_rem[:, :], remT[:, bass.ds(c, 1), :].rearrange("p a u -> p (a u)")).then_inc(slow_add, 1)
                        with v.Fori(0, NW) as w:
                            done = (l * NC + c) * (2 * NW + 1) + w * 2
                            v.wait_ge(slow_add, done + 2)
                            v.tensor_tensor(f_oh[:, :, :], iota[:, :].unsqueeze(1).to_broadcast([P, U, WIN]),
                                            f_rem[:, :].unsqueeze(2).to_broadcast([P, U, WIN]), ALU.is_equal).then_inc(slow_oh, 1)
                            v.wait_ge(slow_oh, (l * NC + c) * NW + w + 1)
                            v.tensor_scalar(f_rem[:, :], f_rem[:, :], float(WIN), None, ALU.subtract).then_inc(slow_add, 1)
                            v.wait_ge(slow_win, (l * NC + c) * NW + w + 1)
                            at = aggT[:, :, bass.ds(w * WIN, WIN)]
                            v.tensor_tensor(at, ps[0][:, 0:KD * WIN].rearrange("p (a b) -> p a b", a=KD), at, ALU.add).then_inc(slow_add, 1)

            def batch_norm(l, base):
                n0 = [0]

                def bstep(ins):
                    ins.then_inc(dve, 1)
                    n0[0] += 1
                    v.wait_ge(dve, base + n0[0])
                bstep(v.tensor_copy(cur[:, :, :], par[:, :, bass.ds(l * KD, KD)]))
                for fo in range(KD):
                    v.wait_ge(mm1_done, l * 4 + fo + 1)
                    for s, (a, w) in enumerate(CUT):
                        bstep(v.bn_stats(stats[:, s, :], ps[2 + 3 * (fo % 2) + s][:, 0:w]))
                    v.sem_inc(stats_ready)
                    bstep(v.bn_aggr(mv[:, fo, :], stats[:, 0:3, :]))
                    bstep(v.tensor_scalar(sc[:, 0, 0:1], mv[:, fo, 1:2], EPS, None, ALU.add))
                    v.sem_inc(root_in)
                    bstep(v.tensor_tensor(sc[:, 7, fo:fo + 1], mv[:, fo, 0:1], cur[:, 0, fo:fo + 1], ALU.add))
                    bstep(v.tensor_tensor(sc[:, 7, fo:fo + 1], cur[:, 0, fo:fo + 1], sc[:, 7, fo:fo + 1], ALU.subtract))
                    v.wait_ge(act_root, l * 4 + fo + 2)
                    bstep(v.reciprocal(sc[:, 2, 0:1], sc[:, 1, 0:1]))
                    bstep(v.scalar_tensor_tensor(out=sc[:, 5, 0:1], in0=sc[:, 0, 0:1], scalar=sc[:, 2, 0:1], in1=sc[:, 2, 0:1], op0=ALU.mult, op1=ALU.mult))
                    bstep(v.tensor_scalar(sc[:, 6, 0:1], sc[:, 5, 0:1], -0.5, 1.5, ALU.mult, ALU.add))
                    bstep(v.scalar_tensor_tensor(out=sc[:, 3, fo:fo + 1], in0=sc[:, 2, 0:1], scalar=sc[:, 6, 0:1], in1=cur[:, 1, fo:fo + 1], op0=ALU.mult, op1=ALU.mult))
                    bstep(v.scalar_tensor_tensor(out=sc[:, 4, fo:fo + 1], in0=sc[:, 7, fo:fo + 1], scalar=sc[:, 3, fo:fo + 1], in1=cur[:, 2, fo:fo + 1], op0=ALU.mult, op1=ALU.add))
                    v.sem_inc(shift_ready)
                return n0[0]

            def attention(c):
                for kind, i in dve_jobs[c]:
                    job(kind, i)

            def job(kind, i):
                if kind == "q":
                    tiles, f = TILES_OF_CUT[i // KD], i % KD
                    w = len(tiles) * P
                    v.wait_ge(mix_exp, i + 1)
                    v.scalar_tensor_tensor(out=mix[:, tiles[0]:tiles[-1] + 1, f * P:(f + 1) * P], in0=by_tile(ps[3 + i % 3][:, 0:w]),
                                           scalar=bq_one[:, f:f + 1], in1=by_tile(att_exp[i % 2][:, 0:w]), op0=ALU.add, op1=ALU.max).then_inc(q_ready, 1)
                if kind == "k":
                    r = rows(i)
                    v.wait_ge(mix_exp, QS + i + 1)
                    v.scalar_tensor_tensor(out=k_rows[0:r, :], in0=ps[3 + i % 2][0:r, :], scalar=1.0, in1=k_rows[0:r, :],
                                           op0=ALU.add, op1=ALU.max).then_inc(k_ready, 1)
                if kind == "v":
                    r = rows(i)
                    if i == 0:
                        step(v.memset(v_rows[:, :, P:], 1.0))
                        v.wait_ge(mixw_loaded, 80)
                    v.wait_ge(kv_done, i) if i > 0 else None
                    v.wait_ge(v_done, i + 1)
                    v.tensor_tensor(v_rows[0:r, :, 0:P], by_tile(ps[5][0:r, :]), by_tile(bv_bc[0:r, :]), ALU.add).then_inc(v_ready, 1)
                if kind == "blocks":
                    v.wait_ge(kv_done, NT)
                    step(v.memset(kvblk[:, :], 0.0))
                    step(v.memset(ksblk[:, :], 0.0))
                    for b in range(2):
                        kvp = ps[6 + b][:, 0:2 * (P + 1)].rearrange("p (a e) -> p a e", e=P + 1)
                        step(v.tensor_copy(ksum[:, 2 * b:2 * b + 2], kvp[:, :, P:].rearrange("p a e -> p (a e)")))
                        for h in range(2):
                            q = slice(h * HD, (h + 1) * HD)
                            step(v.tensor_copy(by_tile(kvblk[q, :])[:, 2 * b:2 * b + 2, q], kvp[q, :, q]))
                            for a in range(2 * b, 2 * b + 2):
                                step(v.tensor_scalar(ksblk[q, a * P + h * HD:a * P + (h + 1) * HD], ones[q, 0:HD], ksum[q, a:a + 1], None, ALU.mult))
                    v.sem_inc(kvblk_ready)
                if kind == "att":
                    tiles, f = TILES_OF_CUT[i // KD], i % KD
                    num, den = nd_banks(i)
                    w = len(tiles) * P
                    v.wait_ge(nd_done, i + 1)
                    if i >= 2:
                        v.wait_ge(att_ready, i - 1)
                    step(v.reciprocal(att_exp[i % 2][:, 0:w], den[:, 0:w]))
                    v.tensor_tensor(mix[:, tiles[0]:tiles[-1] + 1, f * P:(f + 1) * P], by_tile(num[:, 0:w]), by_tile(att_exp[i % 2][:, 0:w]), ALU.mult).then_inc(att_ready, 1)
                if kind == "proj":
                    r = rows(i)
                    v.wait_ge(proj_done, i + 1)
                    if i == 0:
                        v.wait_ge(bp_loaded, 16)
                    step(v.tensor_tensor(mix[0:r, i, :], ps[5][0:r, :], bp_bc[0:r, :], ALU.add))
                    v.wait_ge(xtile_loaded, 16 * (i + 1))
                    step(v.tensor_tensor(mix[0:r, i, :], mix[0:r, i, :], xtile[0:r, :], ALU.add))
                    v.sem_inc(mix_done)

            def stage_rows(l):
                v.wait_ge(be_loaded, l * 16 + 16)
                for t in range(NT):
                    r = rows(t)
                    v.wait_ge(rowT, (l - 1) * NT + t + 1)
                    v.tensor_tensor(xplus[0:r, t, :], ps[t % 2][0:r, :], be_bc[0:r, :], ALU.add).then_inc(staged, 1)
                for k in range(KD):
                    ins = v.tensor_scalar(aggT[:, k, 0:N], xT[:, k, 0:N], eps1[:, bass.ds(l, 1)], None, ALU.mult)
                    ins.then_inc(flushed, 1) if k == KD - 1 else None

            messages(0, attention)
            general(0)
            per = batch_norm(0, n[0])
            n[0] += per
            stage_rows(1)
            messages(1, attention)
            general(1)
            before = n[0]
            batch_norm(1, before)
            with v.Fori(2, L) as l:
                stage_rows(l)
                messages(l, None)
                general(l)
                batch_norm(l, before + (l - 1) * per)
            n[0] = before + (L - 1) * per

            for t in range(NT):
                r = rows(t)
                v.wait_ge(rowT, (L - 1) * NT + t + 1)
                v.tensor_tensor(mix[0:r, t, :], ps[t % 2][0:r, :], mix[0:r, t, :], ALU.add).then_inc(x2_ready, 1)
                v.wait_ge(x2_ready, t + 1)
                step(v.bn_stats(stats[0:r, t, :], mix[0:r, t, :]))
                step(v.bn_aggr(mv[0:r, t, :], stats[0:r, t, :]))
            root_of_var(mv[:, :, 1], NT, L * 4 + 2)
            for t in range(NT):
                r = rows(t)
                v.tensor_scalar(ln_rows[t][0:r, :], mix[0:r, t, :], mv[0:r, t, 0:1], sc[0:r, 3, t:t + 1], ALU.subtract, ALU.mult).then_inc(staged, 1)
            v.wait_ge(router_loaded, 32)
            v.wait_ge(logits_done, NT)
            lgp = ps[6][:, 0:NT * NE].rearrange("p (t e) -> p t e", e=NE)
            lgt = lambda a: lg[:, a, :, :]
            col = lambda a: sc[:, a, :].unsqueeze(2).to_broadcast([P, NT, NE])
            step(v.tensor_tensor(lg[:, 0, 0:NT - 1, :], lgp[:, 0:NT - 1, :], bs_bc[:, :].unsqueeze(1).to_broadcast([P, NT - 1, NE]), ALU.add))
            step(v.memset(lg[:, 0, NT - 1, :], 0.0))
            step(v.tensor_tensor(lg[0:LAST, 0, NT - 1, :], lgp[0:LAST, NT - 1, :], bs_bc[0:LAST, :], ALU.add))
            step(v.tensor_reduce(sc[:, 0, :], lgt(0), AX.X, ALU.max))
            step(v.tensor_tensor(lgt(0), lgt(0), col(0), ALU.subtract))
            v.sem_inc(l_exp_in)
            v.wait_ge(l_exp, 1)
            step(v.tensor_reduce(sc[:, 1, :], lgt(1), AX.X, ALU.add))
            step(v.reciprocal(sc[:, 2, :], sc[:, 1, :]))
            step(v.tensor_tensor(lgt(1), lgt(1), col(2), ALU.mult))
            step(v.tensor_reduce(sc[:, 3, :], lgt(1), AX.X, ALU.max))
            step(v.tensor_tensor(lgt(2), lgt(1), col(3), ALU.is_equal))
            step(v.tensor_scalar(sc[:, 4, 0:NE], iota[:, 0:NE], -1.0, float(NE), ALU.mult, ALU.add))
            step(v.tensor_tensor(lgt(2), lgt(2), sc[:, 4, 0:NE].unsqueeze(1).to_broadcast([P, NT, NE]), ALU.mult))
            step(v.tensor_reduce(sc[:, 5, :], lgt(2), AX.X, ALU.max))
            step(v.tensor_tensor(lgt(2), lgt(2), col(5), ALU.is_equal))
            step(v.tensor_tensor(lgt(2), lgt(2), valid[:, :].unsqueeze(2).to_broadcast([P, NT, NE]), ALU.mult))
            v.sem_inc(gate_ready)

            v.wait_ge(rank_done, 1)
            before_p, total = [ps[b][:, 0:NT * NE].rearrange("p (t e) -> p t e", e=NE) for b in range(2)]
            step(v.memset(lg[:, 3, 0, :], 0.0))
            for t in range(1, NT):
                step(v.tensor_tensor(lg[:, 3, t, :], lg[:, 3, t - 1, :], total[:, t - 1, :], ALU.add))
            tokens, tiles, first, end = [experts[:, m, :] for m in range(4)]
            step(v.tensor_tensor(tokens, lg[:, 3, NT - 1, :], total[:, NT - 1, :], ALU.add))
            step(v.tensor_scalar(rank_of[:, :], count[:, 0:NS], float(P), None, ALU.mult))
            full = compared[:, 0:NE * NT].rearrange("p (e m) -> p e m", e=NE)
            step(v.tensor_tensor(full, tokens.unsqueeze(2).to_broadcast([P, NE, NT]), rank_of[:, 0:NT].unsqueeze(1).to_broadcast([P, NE, NT]), ALU.is_gt))
            step(v.tensor_reduce(tiles, full, AX.X, ALU.add))
            step(v.memset(first, 0.0))
            for e in range(1, NE):
                step(v.tensor_tensor(experts[:, 2, e:e + 1], experts[:, 2, e - 1:e], experts[:, 1, e - 1:e], ALU.add))
            step(v.tensor_tensor(end, first, tiles, ALU.add))
            ended = compared[0:1, 0:NS * NE].rearrange("p (j e) -> p j e", e=NE)
            step(v.tensor_tensor(ended, count[0:1, 0:NS].unsqueeze(2).to_broadcast([1, NS, NE]), experts[0:1, 3, :].unsqueeze(1).to_broadcast([1, NS, NE]), ALU.is_ge))
            step(v.tensor_reduce(left_f[:, 0:NS], ended, AX.X, ALU.add))
            step(v.tensor_scalar(expert_i[:, :], left_f[:, 0:NS], float(NE - 1), None, ALU.min))
            step(v.tensor_tensor(lgt(3), lgt(3), before_p, ALU.add))
            step(v.tensor_tensor(lgt(3), lgt(3), lgt(2), ALU.mult))
            step(v.tensor_reduce(sc[:, 0, :], lgt(3), AX.X, ALU.add))
            step(v.tensor_tensor(lgt(1), lgt(2), first.unsqueeze(1).to_broadcast([P, NT, NE]), ALU.mult))
            step(v.tensor_reduce(sc[:, 1, :], lgt(1), AX.X, ALU.add))
            over = compared[:, 0:NT * (NT - 1)].rearrange("p (t m) -> p t m", t=NT)
            step(v.tensor_tensor(over, sc[:, 0, :].unsqueeze(2).to_broadcast([P, NT, NT - 1]), rank_of[:, 1:NT].unsqueeze(1).to_broadcast([P, NT, NT - 1]), ALU.is_ge))
            step(v.tensor_reduce(sc[:, 2, :], over, AX.X, ALU.add))
            step(v.scalar_tensor_tensor(out=sc[:, 4, :], in0=sc[:, 2, :], scalar=-float(P), in1=sc[:, 0, :], op0=ALU.mult, op1=ALU.add))
            step(v.tensor_tensor(sc[:, 5, :], sc[:, 1, :], sc[:, 2, :], ALU.add))
            step(v.tensor_tensor(place_oh, count[:, :].unsqueeze(1).to_broadcast([P, NT, P]), sc[:, 4, :].unsqueeze(2).to_broadcast([P, NT, P]), ALU.is_equal))
            step(v.tensor_tensor(tile_oh, count[:, 0:NS].unsqueeze(1).to_broadcast([P, NT, NS]), sc[:, 5, :].unsqueeze(2).to_broadcast([P, NT, NS]), ALU.is_equal))
            step(v.tensor_tensor(tile_oh, tile_oh, token[:, :].unsqueeze(2).to_broadcast([P, NT, NS]), ALU.mult))
            v.sem_inc(places_ready)
            step(v.scalar_tensor_tensor(out=slot_i[:, :], in0=sc[:, 5, :], scalar=float(P), in1=sc[:, 4, :], op0=ALU.mult, op1=ALU.add))
            v.wait_ge(token_done, 1)
            step(v.tensor_copy(token_i[:, :], ps[2][:, 0:NS]))
            v.sem_inc(token_ready)

            v.wait_ge(ffn_bias_loaded, 32)
            expert = {}
            for i in range(1, NS + 3):
                if i <= NS:
                    j = i - 1
                    expert[j] = v.value_load(expert_i[0:1, j:j + 1], min_val=0, max_val=NE - 1)
                    v.wait_ge(hid_done, j + 1)
                    if j >= 2:
                        v.wait_ge(hidT_done, j - 1)
                    v.tensor_tensor(hid[j % 2], ps[2 + j % 2][:, 0:F], b1_bc[:, bass.ds(expert[j], 1), :].rearrange("p a f -> p (a f)"), ALU.add).then_inc(hid_sum, 1)
                if 2 <= i <= NS + 1:
                    j = i - 2
                    v.wait_ge(hidT_done, j + 1)
                    if j >= 2:
                        v.wait_ge(y_done, j - 1)
                    v.tensor_copy(hidT[j % 2], ps[4 + j % 2][:, 0:F]).then_inc(hidT_ready, 1)
                if i >= 3:
                    j = i - 3
                    v.wait_ge(y_done, j + 1)
                    if j >= 2:
                        v.wait_ge(y_stored[j % 2], j // 2 * 16)
                    v.tensor_tensor(yrow[j % 2], ps[6 + j % 2][:, :], b2_bc[:, bass.ds(expert[j], 1), :].rearrange("p a d -> p (a d)"), ALU.add).then_inc(y_out, 1)
            for t in range(NT):
                r = rows(t)
                v.wait_ge(yg_got[t], 16)
                v.scalar_tensor_tensor(out=mix[0:r, t, :], in0=ln_rows[t][0:r, :], scalar=sc[0:r, 3, t:t + 1],
                                       in1=mix[0:r, t, :], op0=ALU.mult, op1=ALU.add).then_inc(res_ready, 1)

        @block.scalar
        def _(a):
            def root(s, src, dst):
                a.wait_ge(root_in, s)
                a.activation(dst, src, ACT.Sqrt).then_inc(act_root, 1)

            root(1, sc[:, 0, :], sc[:, 1, :])
            for t in range(NT):
                r = rows(t)
                a.wait_ge(prepT, t + 1)
                a.activation(xT[:, :, t * P:t * P + r], ps[6 + t % 2][:, :].rearrange("p (c n) -> p c n", n=P)[:, :, 0:r], ACT.Copy).then_inc(xnT_ready, 1)
            a.wait_ge(idxT_ready, 1)
            for k in range(STEP):
                a.activation(idx_slot[:, k, :], idxT[:, k, :], ACT.Copy).then_inc(idx_ready, 1)

            def relu(l, k, c, tiles=U):
                a.wait_ge(summed, l * NC + c + 1)
                a.activation(slots[:, k, 0:tiles, :], slots[:, k, 0:tiles, :], ACT.Relu).then_inc(relu_done, 1)

            def parts_copy(l, c, b, groups=G):
                a.wait_ge(parts_done, l * NC + c + STEP + 1)
                a.wait_ge(window_done, l * NC + c + 1)
                q = slice(0, groups * WIN)
                a.activation(parts[q, b, :], ps[b][q, :], ACT.Copy).then_inc(parts_out, 1)

            def message_step(l, i, first=False, beside=None):
                for kk in range(STEP):
                    c = i * STEP + kk
                    relu(l, kk, c)
                    at = idxT[:, bass.ds(c + STEP, 1), :].rearrange("p a u -> p (a u)")
                    a.activation(idx_slot[:, kk, :], at, ACT.Copy).then_inc(idx_ready, 1)
                    if not (first and kk == 0):
                        parts_copy(l, c - 1, (kk + 1) % 2)
                    if beside:
                        beside(l * FULL + c)

            def messages(l, beside):
                if beside:
                    for i in range(ITER):
                        message_step(l, i, first=i == 0, beside=beside)
                else:
                    message_step(l, 0, first=True)
                    with a.Fori(1, ITER) as i:
                        message_step(l, i)
                relu(l, 0, FULL, tiles=1)
                a.wait_ge(relu_done, l * NC + NC)
                a.activation(idx_slot[:, 0, :], idxT[:, 0, :], ACT.Copy).then_inc(idx_ready, 1)
                parts_copy(l, FULL - 1, (FULL - 1) % 2)
                parts_copy(l, FULL, FULL % 2, groups=1)

            def general(l):
                left = a.value_load(left_i[0:1, 0:1], min_val=0, max_val=1)
                with a.If(left > 0):
                    with a.Fori(0, NC) as c:
                        a.wait_ge(idx_ready, l * NC + NC + STEP)
                        a.activation(idx_slot[:, 0, :], idxT[:, bass.ds(c, 1), :].rearrange("p a u -> p (a u)"), ACT.Copy).then_inc(slow_idx, 1)
                        a.wait_ge(slow_sum, l * NC + c + 1)
                        a.activation(slots[:, 0, :, :], slots[:, 0, :, :], ACT.Relu).then_inc(slow_relu, 1)
                        a.wait_ge(slow_win, (l * NC + c + 1) * NW)
                    a.activation(idx_slot[:, 0, :], idxT[:, 0, :], ACT.Copy)

            def dense(l):
                for fo in range(KD):
                    root(l * 4 + fo + 2, sc[:, 0, 0:1], sc[:, 1, 0:1])
                    a.wait_ge(shift_ready, l * 4 + fo + 1)
                    for s, (lo, w) in enumerate(CUT):
                        a.activation(zT[:, fo, lo:lo + w], ps[2 + 3 * (fo % 2) + s][:, 0:w], ACT.Relu,
                                     bias=sc[:, 4, fo:fo + 1], scale=sc[:, 3, fo:fo + 1]).then_inc(z_ready, 1)
                for s, (lo, w) in enumerate(CUT):
                    for fo in range(KD):
                        g = s * KD + fo
                        a.wait_ge(mm2_done, l * 12 + g + 1)
                        a.activation(xT[:, fo, lo:lo + w], ps[2 + g % 6][:, 0:w], ACT.Relu, bias=cur[:, 3, fo:fo + 1]).then_inc(x_ready, 1)

            def attention(c):
                for kind, i in act_jobs[c]:
                    if kind == "q":
                        f, w = i % KD, len(TILES_OF_CUT[i // KD]) * P
                        tmp = att_exp[i % 2][:, 0:w]
                        if i >= 2:
                            a.wait_ge(q_ready, i - 1)
                        a.wait_ge(q_done, i + 1)
                        a.activation(tmp, ps[3 + i % 3][:, 0:w], ACT.Relu, bias=bq_neg[:, f:f + 1], scale=-1.0).then_inc(mix_t, 1)
                        a.wait_ge(mix_t, i + 1)
                        a.activation(tmp, tmp, ACT.Exp, scale=-1.0).then_inc(mix_exp, 1)
                    if kind == "k":
                        tmp = k_rows[0:rows(i), :]
                        a.wait_ge(q_ready, QS) if i == 0 else a.wait_ge(kv_done, i)
                        a.wait_ge(k_done, i + 1)
                        a.activation(tmp, ps[3 + i % 2][0:rows(i), :], ACT.Relu, scale=-1.0).then_inc(mix_t, 1)
                        a.wait_ge(mix_t, QS + i + 1)
                        a.activation(tmp, tmp, ACT.Exp, scale=-1.0).then_inc(mix_exp, 1)

            messages(0, attention)
            general(0)
            dense(0)
            messages(1, attention)
            general(1)
            dense(1)
            with a.Fori(2, L) as l:
                messages(l, None)
                general(l)
                dense(l)

            root(L * 4 + 2, sc[:, 0, :], sc[:, 1, :])
            for t in range(NT):
                r = rows(t)
                a.wait_ge(lnT, t + 1)
                a.activation(zT[:, :, t * P:t * P + r], ps[2 + t % 2][:, :].rearrange("p (c n) -> p c n", n=P)[:, :, 0:r], ACT.Copy).then_inc(lnT_out, 1)
            a.wait_ge(l_exp_in, 1)
            a.activation(lg[:, 1, :, :], lg[:, 0, :, :], ACT.Exp).then_inc(l_exp, 1)
            for i in range(NS + 1):
                if i < NS:
                    a.wait_ge(xgT_done, i + 1)
                    if i >= 2:
                        a.wait_ge(hid_done, i - 1)
                    a.activation(xgT[i % 2], ps[i % 2][:, :], ACT.Copy).then_inc(xgT_ready, 1)
                if i >= 1:
                    j = i - 1
                    a.wait_ge(hid_sum, j + 1)
                    a.activation(hid[j % 2], hid[j % 2], ACT.Gelu).then_inc(hid_ready, 1)

        @block.tensor
        def _(pe):
            def mm(o, lhsT, rhs, start, stop):
                return nc.tensor.matmul(o, lhsT, rhs, start=start, stop=stop)

            for _ in range(STEP):
                pe.sem_inc(parts_done)
            for _ in range(2):
                pe.sem_inc(parts_out)
                pe.sem_inc(window_done)
            pe.wait_ge(ident_ready, 1)
            pe.wait_ge(src_ready, 1)
            for u in range(U):
                ins = pe.transpose(ps[0][:, u * NC:(u + 1) * NC], edge_rows[:, 3, u * P:(u + 1) * P], ident[0:NC, 0:NC])
            ins.then_inc(edgeT, 1)
            for t in range(NT):
                r = rows(t)
                pe.wait_ge(ln_ready, t + 1)
                if t >= 2:
                    pe.wait_ge(xnT_ready, t - 1)
                for c in range(KD):
                    ins = pe.transpose(ps[6 + t % 2][:, c * P:c * P + r], xrow[0:r, t, c * P:(c + 1) * P], ident[0:r, 0:r])
                ins.then_inc(prepT, 1)
            pe.wait_ge(edges_ready, 1)
            for m, row in ((1, 2), (2, 5), (3, 0)):
                for u in range(U):
                    ins = pe.transpose(ps[m][:, u * NC:(u + 1) * NC], edge_rows[:, row, u * P:(u + 1) * P], ident[0:NC, 0:NC])
                ins.then_inc(edgeT, 1)
            pe.transpose(ps[4][0:1, 0:NC], edge_sc[:, 0:1], ident[0:NC, 0:NC])
            pe.transpose(ps[4][0:1, P:P + NC], edge_sc[:, 1:2], ident[0:NC, 0:NC])
            pe.wait_ge(small_loaded, 112)
            pe.transpose(ps[5][:, 0:ALLPAR], params_row[:, :], ident[0:ALLPAR, 0:ALLPAR]).then_inc(edgeT, 1)
            pe.wait_ge(prep_done, 1)

            def group_sums(l, k, b, c, tiles=U):
                pe.wait_ge(relu_done, l * NC + c + 1)
                pe.wait_ge(parts_out, l * NC + c + 1)
                for u in range(tiles):
                    g = u % G
                    ins = mm(ps[b][g * WIN:(g + 1) * WIN, :], onehot[:, k, u, :],
                             slots[:, k, u, :], u < G, u + G >= tiles)
                ins.then_inc(parts_done, 1)

            def fold_groups(l, b, c, groups=G):
                pe.wait_ge(parts_out, l * NC + c + 3)
                pe.wait_ge(flushed, l * (NC + 1) + c + 3)
                q = slice(0, groups * WIN)
                for m in range(KD):
                    ins = mm(ps[2][:, m * WIN:(m + 1) * WIN], parts[q, b, m * P:(m + 1) * P], fold[q, :], True, True)
                ins.then_inc(window_done, 1)

            def message_step(l, i, first=False, beside=None):
                for kk in range(STEP):
                    c = i * STEP + kk
                    if beside:
                        beside(l * FULL + c)
                    group_sums(l, kk, kk % 2, c)
                    if not (first and kk == 0):
                        fold_groups(l, (kk + 1) % 2, c - 1)

            def messages(l, beside):
                if beside:
                    for i in range(ITER):
                        message_step(l, i, first=i == 0, beside=beside)
                else:
                    message_step(l, 0, first=True)
                    with pe.Fori(1, ITER) as i:
                        message_step(l, i)
                group_sums(l, 0, FULL % 2, FULL, tiles=1)
                fold_groups(l, (FULL - 1) % 2, FULL - 1)
                fold_groups(l, FULL % 2, FULL, groups=1)

            def general(l):
                left = pe.value_load(left_i[0:1, 0:1], min_val=0, max_val=1)
                with pe.If(left > 0):
                    with pe.Fori(0, NC) as c:
                        pe.wait_ge(slow_relu, l * NC + c + 1)
                        pe.sem_inc(slow_go)
                        with pe.Fori(0, NW) as w:
                            pe.wait_ge(slow_oh, (l * NC + c) * NW + w + 1)
                            for q in range(KD):
                                for u in range(U):
                                    ins = mm(ps[0][:, q * WIN:(q + 1) * WIN], slots[:, 0, u, q * P:(q + 1) * P], f_oh[:, u, :], u == 0, u == U - 1)
                            ins.then_inc(slow_win, 1)
                    pe.wait_ge(slow_add, (l + 1) * NC * (2 * NW + 1) + 1)

            def key_value(t):
                r = rows(t)
                pe.wait_ge(k_ready, t + 1)
                pe.wait_ge(v_ready, t + 1)
                for c in range(KD):
                    at = slice(c % 2 * (P + 1), (c % 2 + 1) * (P + 1))
                    ins = mm(ps[6 + c // 2][:, at], k_rows[0:r, c * P:(c + 1) * P], v_rows[0:r, c, :], t == 0 and c % 2 == 0, t == NT - 1 and c % 2 == 1)
                ins.then_inc(kv_done, 1)

            def attention(c):
                for kind, i in pe_jobs[c]:
                    job(kind, i)

            def job(kind, i):
                if kind == "q":
                    tiles, f = TILES_OF_CUT[i // KD], i % KD
                    lo, w = tiles[0] * P, len(tiles) * P
                    if i == 0:
                        pe.wait_ge(mixw_loaded, 80)
                    if i >= 3:
                        pe.wait_ge(q_ready, i - 2)
                    for k in range(KD):
                        ins = mm(ps[3 + i % 3][:, 0:w], wq[:, k, f * P:(f + 1) * P], xT[:, k, lo:lo + w], k == 0, k == KD - 1)
                    ins.then_inc(q_done, 1)
                if kind == "k":
                    r = rows(i)
                    if i == 0:
                        pe.wait_ge(q_ready, QS)
                    if i >= 2:
                        pe.wait_ge(k_ready, i - 1)
                    for k in range(KD):
                        mm(ps[3 + i % 2][0:r, :], xT[:, k, i * P:i * P + r], wk[:, k, :], k == 0, False)
                    mm(ps[3 + i % 2][0:r, :], ones[0:1, 0:r], k_bias, False, True).then_inc(k_done, 1)
                if kind == "v":
                    r = rows(i)
                    if i > 0:
                        pe.wait_ge(v_ready, i)
                    for k in range(KD):
                        ins = mm(ps[5][0:r, :], xT[:, k, i * P:i * P + r], wv[:, k, :], k == 0, k == KD - 1)
                    ins.then_inc(v_done, 1)
                if kind == "kv":
                    key_value(i)
                if kind == "att":
                    tiles, f = TILES_OF_CUT[i // KD], i % KD
                    num, den = nd_banks(i)
                    w = len(tiles) * P
                    if i == 0:
                        pe.wait_ge(kvblk_ready, 1)
                    if i >= 2:
                        pe.wait_ge(att_ready, i - 1)
                    qT = mix[:, tiles[0]:tiles[-1] + 1, f * P:(f + 1) * P]
                    mm(by_tile(num[:, 0:w]), kvblk[:, f * P:(f + 1) * P], qT, True, True)
                    mm(by_tile(den[:, 0:w]), ksblk[:, f * P:(f + 1) * P], qT, True, True).then_inc(nd_done, 1)
                if kind == "proj":
                    r = rows(i)
                    if i == 0:
                        pe.wait_ge(wp_loaded, 16)
                    else:
                        pe.wait_ge(mix_done, i)
                    pe.wait_ge(att_ready, KD * (i // 4 + 1))
                    for k in range(KD):
                        ins = mm(ps[5][0:r, :], mix[:, i, k * P:k * P + r], wp[:, k, :], k == 0, k == KD - 1)
                    ins.then_inc(proj_done, 1)

            def dense(l):
                pe.wait_ge(flushed, (l + 1) * (NC + 1) + 2)
                pe.wait_ge(w1_loaded, l * 16 + 16)
                for fo in range(KD):
                    if fo >= 2:
                        pe.wait_ge(z_ready, l * 12 + 3 * (fo - 1))
                    for k in range(KD):
                        for s, (lo, w) in enumerate(CUT):
                            ins = mm(ps[2 + 3 * (fo % 2) + s][:, 0:w], w1[:, k, fo * P:(fo + 1) * P], aggT[:, k, lo:lo + w], k == 0, k == KD - 1)
                    ins.then_inc(mm1_done, 1)
                pe.wait_ge(w2_loaded, l * 16 + 16)

                def second(g, ks):
                    s, fo = g // KD, g % KD
                    lo, w = CUT[s]
                    for k in ks:
                        ins = mm(ps[2 + g % 6][:, 0:w], w2[:, k, fo * P:(fo + 1) * P], zT[:, k, lo:lo + w], k == 0, k == KD - 1)
                        if k == KD - 1:
                            ins.then_inc(mm2_done, 1)

                pe.wait_ge(z_ready, l * 12 + 9)
                for g in range(3):
                    second(g, range(KD - 1))
                pe.wait_ge(z_ready, (l + 1) * 12)
                for g in range(len(CUT) * KD):
                    if g < 3:
                        second(g, [KD - 1])
                        continue
                    if g >= 6:
                        pe.wait_ge(x_ready, l * 12 + g - 5)
                    second(g, range(KD))
                    if g % KD == 0:
                        rows_of(l, g // KD - 1)
                rows_of(l, len(CUT) - 1)

            def rows_of(l, s):
                pe.wait_ge(x_ready, l * 12 + (s + 1) * KD)
                for t in TILES_OF_CUT[s]:
                    r = rows(t)
                    if t >= 2:
                        free_rows(l, t)
                    for c in range(KD):
                        ins = pe.transpose(ps[t % 2][0:r, c * P:(c + 1) * P], xT[:, c, t * P:t * P + r], ident[:, :])
                    ins.then_inc(rowT, 1)

            def free_rows(l, t):
                if last[0]:
                    pe.wait_ge(x2_ready, t - 1)
                else:
                    pe.wait_ge(staged, l * NT + t - 1)

            last = [False]
            messages(0, attention)
            general(0)
            dense(0)
            messages(1, attention)
            general(1)
            dense(1)
            with pe.Fori(2, L - 1) as l:
                messages(l, None)
                general(l)
                dense(l)
            last[0] = True
            messages(L - 1, None)
            general(L - 1)
            dense(L - 1)

            pe.wait_ge(router_loaded, 32)
            for t in range(NT):
                r = rows(t)
                pe.wait_ge(staged, (L - 1) * NT + t + 1)
                if t >= 2:
                    pe.wait_ge(lnT_out, t - 1)
                for c in range(KD):
                    ins = pe.transpose(ps[2 + t % 2][:, c * P:c * P + r], ln_rows[t][0:r, c * P:(c + 1) * P], ident[0:r, 0:r])
                ins.then_inc(lnT, 1)
            for t in range(NT):
                r = rows(t)
                pe.wait_ge(lnT_out, t + 1)
                for k in range(KD):
                    ins = mm(ps[6][0:r, t * NE:(t + 1) * NE], zT[:, k, t * P:t * P + r], ws[:, k, :], k == 0, k == KD - 1)
                ins.then_inc(logits_done, 1)

            pe.wait_ge(gate_ready, 1)
            pe.wait_ge(consts_made, 6)
            routed = lg[:, 2, :, :].rearrange("p t e -> p (t e)")
            mm(ps[0][:, 0:NT * NE], tri[:, :], routed, True, True)
            mm(ps[1][:, 0:NT * NE], ones[:, :], routed, True, True).then_inc(rank_done, 1)
            pe.wait_ge(places_ready, 1)
            for t in range(NT):
                ins = mm(ps[2][:, 0:NS], place_oh[:, t, :], tile_oh[:, t, :], t == 0, t == NT - 1)
            ins.then_inc(token_done, 1)

            pe.wait_ge(ffn_loaded, 2 * NE * 16)
            pe.wait_ge(token_ready, 1)
            expert = {}
            for i in range(NS + 3):
                if i < NS:
                    expert[i] = pe.value_load(expert_i[0:1, i:i + 1], min_val=0, max_val=NE - 1)
                    pe.wait_ge(xg_got[i % 4], 16 * (i // 4 + 1))
                    if i >= 2:
                        pe.wait_ge(xgT_ready, i - 1)
                    for c in range(KD):
                        ins = pe.transpose(ps[i % 2][:, c * P:(c + 1) * P], xg[i % 4][:, c * P:(c + 1) * P], ident[:, :])
                    ins.then_inc(xgT_done, 1)
                if 1 <= i <= NS:
                    j = i - 1
                    pe.wait_ge(xgT_ready, j + 1)
                    if j >= 2:
                        pe.wait_ge(hid_sum, j - 1)
                    o = ps[2 + j % 2][:, 0:F]
                    for k in range(KD):
                        ins = mm(o, xgT[j % 2][:, k * P:(k + 1) * P], ew1[:, bass.ds(expert[j], 1), k, :].rearrange("p a f -> p (a f)"), k == 0, k == KD - 1)
                    ins.then_inc(hid_done, 1)
                if 2 <= i <= NS + 1:
                    j = i - 2
                    pe.wait_ge(hid_ready, j + 1)
                    if j >= 2:
                        pe.wait_ge(hidT_ready, j - 1)
                    for f in range(KF):
                        ins = pe.transpose(ps[4 + j % 2][:, f * P:(f + 1) * P], hid[j % 2][:, f * P:(f + 1) * P], ident[:, :])
                    ins.then_inc(hidT_done, 1)
                if i >= 3:
                    j = i - 3
                    pe.wait_ge(hidT_ready, j + 1)
                    if j >= 2:
                        pe.wait_ge(y_out, j - 1)
                    for f in range(KF):
                        ins = mm(ps[6 + j % 2][:, :], hidT[j % 2][:, f * P:(f + 1) * P], ew2[:, bass.ds(expert[j], 1), f, :].rearrange("p a d -> p (a d)"), f == 0, f == KF - 1)
                    ins.then_inc(y_done, 1)


def kernel(**inputs):
    import numpy as _np
    import concourse.bacc as _bacc
    from concourse import mybir as _mybir
    from concourse.bass_utils import run_bass_kernel_spmd as _run

    nc = _bacc.Bacc("TRN2", target_bir_lowering=False, num_devices=1)
    arrays, io = {}, {}
    for name in inputs:
        a = _np.ascontiguousarray(inputs[name])
        arrays[f"in_{name}"] = a
        io[name] = nc.dram_tensor(f"in_{name}", a.shape, _mybir.dt.from_np(a.dtype), kind="ExternalInput").ap()
    shape = inputs["x"].shape
    out = nc.dram_tensor("out_0", shape, _mybir.dt.float32, kind="ExternalOutput").ap()
    build_gps_block(nc, io, out)
    r = _run(nc, [arrays], core_ids=[0])
    return r.results[0]["out_0"]
```
